# Optimizing a Trainium2 kernel written in Bass

```python
import numpy as np
import jax
import jax.numpy as jnp

def _softmax(x, axis=-1):
    return jax.nn.softmax(x, axis=axis)

def _gelu(x):
    return jax.nn.gelu(x, approximate=True)

def _silu(x):
    return jax.nn.silu(x)

def _sigmoid(x):
    return jax.nn.sigmoid(x)

def _layernorm(x, axis=-1, eps=1e-05):
    m = jnp.mean(x, axis=axis, keepdims=True)
    v = jnp.var(x, axis=axis, keepdims=True)
    return (x - m) / jnp.sqrt(v + eps)

def _scatter_add(tgt, idx, src, axis=0):
    return tgt.at[idx].add(src)

def _segment_sum(src, seg, n):
    return jax.ops.segment_sum(src, seg, n)
kernel_name = 'mk_adj_ffn_d2_adj_r2_0c82df'

def setup_inputs(seed: int=0):
    np.random.seed(seed)
    _w = jnp.asarray

    def _rec_inputs():
        import jax
        import jax.numpy as jnp
        _gk = jax.random.key(seed)
        x = -0.0005146 + 1 * jax.random.normal(jax.random.fold_in(_gk, 1), (8, 1024, 128), jnp.float32)
        _w = (1.0 + jnp.arange(1024, dtype=jnp.float32)) ** (-0.5)
        _w = _w / _w.mean()
        _pij = jnp.clip(0.00390625 * _w[:, None] * _w[None, :], 0.0, 1.0)
        _a = jax.random.uniform(jax.random.fold_in(_gk, 2), (8, 1024, 1024)) < _pij
        adj = _a.astype(jnp.int32)
        return (x, adj)
    x, adj = _rec_inputs()

    def _L0_gnn_setup():
        import jax, jax.numpy as jnp
        import numpy as np
        B, N, C, OUT, S = (4, 1024, 128, 128, 25)
        DENSITY = 0.008
        key = jax.random.key(seed)
        kA, kX, kW = jax.random.split(key, 3)
        A = jax.random.bernoulli(kA, DENSITY, (B, N, N)).astype(jnp.int32)
        X = jax.random.normal(kX, (B, N, C), dtype=jnp.float32)
        W = jax.random.normal(kW, (2 * C, OUT), dtype=jnp.float32) * np.float32(1.0 / np.sqrt(2 * C))
        b = jnp.zeros((OUT,), dtype=jnp.float32)
        return {'A': A, 'X': X, 'W': W, 'b': b}
    _L0_gnn_all = _L0_gnn_setup()
    _L0_gnn_in = {k: v for k, v in _L0_gnn_all.items() if k in ('W', 'b')}
    del _L0_gnn_all

    def _L0_ffn_setup():
        import jax, jax.numpy as jnp
        import numpy as np
        TOP_K = 2
        key = jax.random.key(seed)
        ks = jax.random.split(key, 4)
        B, L, D, H, E = (8, 2048, 128, 512, 8)
        s = 0.02
        return {'x': jax.random.normal(ks[0], (B, L, D), jnp.float32), 'Wg': jax.random.normal(ks[1], (D, E), jnp.float32) * s, 'bg': jnp.zeros((E,), jnp.float32), 'W1': jax.random.normal(ks[2], (E, D, H), jnp.float32) * s, 'b1': jnp.zeros((E, H), jnp.float32), 'W2': jax.random.normal(ks[3], (E, H, D), jnp.float32) * s, 'b2': jnp.zeros((E, D), jnp.float32)}
    _L0_ffn_all = _L0_ffn_setup()
    _L0_ffn_in = {k: v for k, v in _L0_ffn_all.items() if k in ('Wg', 'bg', 'W1', 'b1', 'W2', 'b2')}
    del _L0_ffn_all

    def _L1_gnn_setup():
        import jax, jax.numpy as jnp
        import numpy as np
        UNITS = 128
        NUM_HEADS = 8
        HEAD_DIM = UNITS // NUM_HEADS
        B, N = (8, 1024)
        key = jax.random.key(seed)
        ks = jax.random.split(key, 7)
        node_features = jax.random.normal(ks[0], (B, N, UNITS), dtype=jnp.float32)
        adjacency_matrix = jax.random.randint(ks[1], (B, N, N), 0, 2, dtype=jnp.int32)
        s = 1.0 / np.sqrt(UNITS)
        Wq = jax.random.normal(ks[2], (UNITS, UNITS), dtype=jnp.float32) * s
        Wk = jax.random.normal(ks[3], (UNITS, UNITS), dtype=jnp.float32) * s
        Wv = jax.random.normal(ks[4], (UNITS, UNITS), dtype=jnp.float32) * s
        Wo = jax.random.normal(ks[5], (UNITS, UNITS), dtype=jnp.float32) * s
        bo = jnp.zeros((UNITS,), dtype=jnp.float32)
        return {'node_features': node_features, 'adjacency_matrix': adjacency_matrix, 'Wq': Wq, 'Wk': Wk, 'Wv': Wv, 'Wo': Wo, 'bo': bo}
    _L1_gnn_all = _L1_gnn_setup()
    _L1_gnn_in = {k: v for k, v in _L1_gnn_all.items() if k in ('Wq', 'Wk', 'Wv', 'Wo', 'bo')}
    del _L1_gnn_all

    def _L1_ffn_setup():
        import jax, jax.numpy as jnp
        import numpy as np
        E, D, H, TOP_K = (6, 128, 128, 2)
        ROUTER_H = D // 2
        key = jax.random.key(seed)
        ks = jax.random.split(key, 12)
        s = 1.0 / np.sqrt(D)
        sh = 1.0 / np.sqrt(H)
        sr = 1.0 / np.sqrt(ROUTER_H)
        return {'features': jax.random.normal(ks[0], (8, 2048, D), dtype=jnp.float32), 'router_w1': jax.random.uniform(ks[1], (D, ROUTER_H), jnp.float32, -s, s), 'router_b1': jnp.zeros((ROUTER_H,), jnp.float32), 'router_w2': jax.random.uniform(ks[2], (ROUTER_H, E), jnp.float32, -sr, sr), 'router_b2': jnp.zeros((E,), jnp.float32), 'expert_w1': jax.random.uniform(ks[3], (E, D, H), jnp.float32, -s, s), 'expert_b1': jnp.zeros((E, H), jnp.float32), 'expert_w2': jax.random.uniform(ks[4], (E, H, H), jnp.float32, -sh, sh), 'expert_b2': jnp.zeros((E, H), jnp.float32), 'expert_w3': jax.random.uniform(ks[5], (E, H, D), jnp.float32, -sh, sh), 'expert_b3': jnp.zeros((E, D), jnp.float32)}
    _L1_ffn_all = _L1_ffn_setup()
    _L1_ffn_in = {k: v for k, v in _L1_ffn_all.items() if k in ('router_w1', 'router_b1', 'router_w2', 'router_b2', 'expert_w1', 'expert_b1', 'expert_w2', 'expert_b2', 'expert_w3', 'expert_b3')}
    del _L1_ffn_all
    return {'x': x, 'adj': adj, 'L0_gnn_W': _L0_gnn_in['W'], 'L0_gnn_b': _L0_gnn_in['b'], 'L0_ffn_Wg': _L0_ffn_in['Wg'], 'L0_ffn_bg': _L0_ffn_in['bg'], 'L0_ffn_W1': _L0_ffn_in['W1'], 'L0_ffn_b1': _L0_ffn_in['b1'], 'L0_ffn_W2': _L0_ffn_in['W2'], 'L0_ffn_b2': _L0_ffn_in['b2'], 'L1_gnn_Wq': _L1_gnn_in['Wq'], 'L1_gnn_Wk': _L1_gnn_in['Wk'], 'L1_gnn_Wv': _L1_gnn_in['Wv'], 'L1_gnn_Wo': _L1_gnn_in['Wo'], 'L1_gnn_bo': _L1_gnn_in['bo'], 'L1_ffn_router_w1': _L1_ffn_in['router_w1'], 'L1_ffn_router_b1': _L1_ffn_in['router_b1'], 'L1_ffn_router_w2': _L1_ffn_in['router_w2'], 'L1_ffn_router_b2': _L1_ffn_in['router_b2'], 'L1_ffn_expert_w1': _L1_ffn_in['expert_w1'], 'L1_ffn_expert_b1': _L1_ffn_in['expert_b1'], 'L1_ffn_expert_w2': _L1_ffn_in['expert_w2'], 'L1_ffn_expert_b2': _L1_ffn_in['expert_b2'], 'L1_ffn_expert_w3': _L1_ffn_in['expert_w3'], 'L1_ffn_expert_b3': _L1_ffn_in['expert_b3']}

def reference(x, adj, L0_gnn_W, L0_gnn_b, L0_ffn_Wg, L0_ffn_bg, L0_ffn_W1, L0_ffn_b1, L0_ffn_W2, L0_ffn_b2, L1_gnn_Wq, L1_gnn_Wk, L1_gnn_Wv, L1_gnn_Wo, L1_gnn_bo, L1_ffn_router_w1, L1_ffn_router_b1, L1_ffn_router_w2, L1_ffn_router_b2, L1_ffn_expert_w1, L1_ffn_expert_b1, L1_ffn_expert_w2, L1_ffn_expert_b2, L1_ffn_expert_w3, L1_ffn_expert_b3):
    import jax
    import jax.numpy as jnp

    def _L0_gnn_ref(A, X, W, b):
        import jax, jax.numpy as jnp
        import numpy as np
        B, N, C, OUT, S = (4, 1024, 128, 128, 25)
        DENSITY = 0.008
        mask = A != 0
        neg_inf = jnp.float32(-jnp.inf)
        pri = -jnp.arange(N, dtype=jnp.float32)
        scores = jnp.where(mask, pri, neg_inf)
        vals, idx = jax.lax.top_k(scores, S)
        valid = vals > neg_inf
        feats = jax.vmap(lambda x, i: x[i])(X, idx)
        feats = jnp.where(valid[..., None], feats, neg_inf)
        agg = feats.max(axis=2)
        degree = mask.sum(axis=-1)
        agg = jnp.where((degree <= S)[..., None], jnp.maximum(agg, 0.0), agg)
        h = jnp.concatenate([X, agg], axis=-1)
        out = jax.nn.relu(jnp.einsum('bnf,fo->bno', h, W) + b)
        return out

    def _L0_ffn_ref(x, Wg, bg, W1, b1, W2, b2):
        import jax, jax.numpy as jnp
        import numpy as np
        TOP_K = 2
        B, L, D = x.shape
        E = W1.shape[0]
        xf = x.reshape(-1, D)
        gate_logits = xf @ Wg + bg
        top_w, top_i = jax.lax.top_k(gate_logits, TOP_K)
        top_w = jax.nn.softmax(top_w, axis=-1)
        w_dense = jnp.sum(jax.nn.one_hot(top_i, E, dtype=xf.dtype) * top_w[..., None], axis=1)
        out = jnp.zeros_like(xf)
        for e in range(E):
            h = jax.nn.gelu(xf @ W1[e] + b1[e], approximate=False)
            out = out + w_dense[:, e:e + 1] * (h @ W2[e] + b2[e])
        return out.reshape(B, L, D)

    def _L1_gnn_ref(node_features, adjacency_matrix, Wq, Wk, Wv, Wo, bo):
        import jax, jax.numpy as jnp
        import numpy as np
        UNITS = 128
        NUM_HEADS = 8
        HEAD_DIM = UNITS // NUM_HEADS
        B, N = (8, 1024)
        b, n, _ = node_features.shape
        h, d = (NUM_HEADS, HEAD_DIM)
        q = (node_features @ Wq).reshape(b, n, h, d).transpose(0, 2, 1, 3)
        k = (node_features @ Wk).reshape(b, n, h, d).transpose(0, 2, 1, 3)
        v = (node_features @ Wv).reshape(b, n, h, d).transpose(0, 2, 1, 3)
        scores = jnp.einsum('bhqd,bhkd->bhqk', q, k) / jnp.sqrt(jnp.float32(d))
        mask = adjacency_matrix[:, None, :, :] > 0
        scores = jnp.where(mask, scores, jnp.float32(-1000000000.0))
        w = jax.nn.softmax(scores, axis=-1)
        ctx = jnp.einsum('bhqk,bhkd->bhqd', w, v)
        ctx = ctx.transpose(0, 2, 1, 3).reshape(b, n, h * d)
        return ctx @ Wo + bo

    def _L1_ffn_ref(features, router_w1, router_b1, router_w2, router_b2, expert_w1, expert_b1, expert_w2, expert_b2, expert_w3, expert_b3):
        import jax, jax.numpy as jnp
        import numpy as np
        E, D, H, TOP_K = (6, 128, 128, 2)
        ROUTER_H = D // 2
        rh = jax.nn.relu(features @ router_w1 + router_b1)
        expert_logits = jax.nn.softmax(rh @ router_w2 + router_b2, axis=-1)
        top_w, top_i = jax.lax.top_k(expert_logits, TOP_K)
        routing_weights = jax.nn.softmax(top_w, axis=-1)
        h1 = jax.nn.relu(jnp.einsum('bsd,edh->bseh', features, expert_w1) + expert_b1)
        h2 = jax.nn.relu(jnp.einsum('bseh,ehf->bsef', h1, expert_w2) + expert_b2)
        expert_out = jnp.einsum('bsef,efo->bseo', h2, expert_w3) + expert_b3
        sel = jnp.take_along_axis(expert_out, top_i[:, :, :, None], axis=2)
        combined = jnp.sum(sel * routing_weights[..., None], axis=2)
        return combined
    x = x + _L0_gnn_ref(adj, _layernorm(x, axis=-1), L0_gnn_W, L0_gnn_b)
    x = x + _L0_ffn_ref(_layernorm(x, axis=-1), L0_ffn_Wg, L0_ffn_bg, L0_ffn_W1, L0_ffn_b1, L0_ffn_W2, L0_ffn_b2)
    x = x + _L1_gnn_ref(_layernorm(x, axis=-1), adj, L1_gnn_Wq, L1_gnn_Wk, L1_gnn_Wv, L1_gnn_Wo, L1_gnn_bo)
    x = x + _L1_ffn_ref(_layernorm(x, axis=-1), L1_ffn_router_w1, L1_ffn_router_b1, L1_ffn_router_w2, L1_ffn_router_b2, L1_ffn_expert_w1, L1_ffn_expert_b1, L1_ffn_expert_w2, L1_ffn_expert_b2, L1_ffn_expert_w3, L1_ffn_expert_b3)
    return x

_drawn_inputs = setup_inputs


def setup_inputs(seed=0):
    import zlib

    import numpy as np

    out = dict(_drawn_inputs(seed))
    spreads = {'L0_gnn_b': (0.0, 0.1),
     'L0_ffn_bg': (0.0, 0.1),
     'L0_ffn_b1': (0.0, 0.433),
     'L0_ffn_b2': (0.0, 0.1),
     'L1_gnn_bo': (0.0, 0.1),
     'L1_ffn_router_b1': (0.0, 0.1),
     'L1_ffn_router_b2': (0.0, 0.276),
     'L1_ffn_expert_b1': (0.0, 0.8),
     'L1_ffn_expert_b2': (0.0, 0.38),
     'L1_ffn_expert_b3': (0.0, 0.1)}
    factors = {}
    for name, (base, spread) in spreads.items():
        noise = np.random.default_rng([zlib.crc32(name.encode()), seed]).standard_normal(out[name].shape)
        drawn = base * np.exp(spread * noise) if base else spread * noise
        out[name] = jnp.asarray(drawn.astype(out[name].dtype))
    for name, factor in factors.items():
        out[name] = (out[name] * factor).astype(out[name].dtype)
    return out
```

```python
from contextlib import ExitStack

import concourse.bass as bass
from concourse import mybir

F32 = mybir.dt.float32
BF16 = mybir.dt.bfloat16
F16 = mybir.dt.float16
U8 = mybir.dt.uint8
I32 = mybir.dt.int32
U32 = mybir.dt.uint32
ALU = mybir.AluOpType
ACT = mybir.ActivationFunctionType
AX = mybir.AxisListType

GRAPHS, NODES, C = 8, 1024, 128
P = 128
TILES = NODES // P
HALF = 512
HTILES = HALF // P
SLOTS = 25
TOP = 32
ROUNDS = TOP // 8
ROWS = NODES + 1
E0, HID0 = 8, 512
HC = HID0 // P
E1, RH = 6, 64
EP = 8
HEADS, D = 8, 16
PARTS = 3
PAIRS = 6
QPART = [0, 1, 0, 1, 2, 0]
KPART = [0, 0, 1, 1, 0, 2]
SROWS = PAIRS * D
GH = 4
BIG = float(2 ** 30)
LOWEST = -3.0e38
EPS = 1e-5


def psum_plan():
    one = []
    for hf in range(2):
        one += [("xn", hf), ("agg", hf), ("gnn", hf)]
    one += [("t0", 0), ("t0", 1), ("b0", 0), ("b0", 1)]
    order0 = [(hf, e) for hf in range(2) for e in range(E0)]
    one += [("h0", hf, e, c) for hf, e in order0 for c in range(HC)]
    for name in ("ta", "tq", "q", "k", "v"):
        one += [(name, 0), (name, 1)]
    for qh in range(2):
        one += [("ctx", qh, 0), ("ctx", qh, 1), ("ctxT", qh), ("proj", qh)]
    one += [("t1", 0), ("t1", 1), ("r1", 0), ("r1", 1), ("b1", 0), ("b1", 1)]
    order1 = [(hf, e) for hf in range(2) for e in range(E1)]
    for i in range(len(order1) + 1):
        if i < len(order1):
            one.append(("u1", *order1[i]))
        if i >= 1:
            one.append(("u2", *order1[i - 1]))
    two = [("s", t, h) for t in range(TILES) for h in range(HEADS)]
    two += [("st", qh, g, kc, pr) for qh in range(2) for g in range(2) for kc in range(TILES) for pr in range(2)]
    acc = [("y0", hf, e) for hf, e in order0]
    acc += [("av", qh, g) for qh in range(2) for g in range(2)]
    acc += [("y1", hf, e) for hf, e in order1]
    misc = ["lg0", "wT0", "mT", "lg1", "wT1"]
    place, uses = {}, {}
    for name, ring, banks in (("H", one, 2), ("A", two, 2), ("Y", acc, 1), ("M", misc, 1)):
        assert len(ring) % banks == 0
        uses[name] = len(ring) // banks
        for i, key in enumerate(ring):
            place[key] = (name, i % banks, i // banks)
    return place, uses, order0, order1


def graph_kernel(nc, x, adj, gW, gb, Wg, bg, W1, b1, W2, b2, Wq, Wk, Wv, Wo, bo,
                 rw1, rb1, rw2, rb2, ew1, eb1, ew2, eb2, ew3, eb3, out):
    PLACE, USES, ORDER0, ORDER1 = psum_plan()
    ctx = ExitStack()
    with ctx:
        def sb(name, shape, dt=F32):
            return ctx.enter_context(nc.sbuf_tensor(name, shape, dt))

        def sem(name):
            return ctx.enter_context(nc.semaphore(name))

        table = nc.dram_tensor("table", (ROWS, C), F32, kind="Internal").ap()
        parts_dram = nc.dram_tensor("parts_dram", (2, PARTS, P, NODES), BF16, kind="Internal").ap()

        gW_sb = sb("gW_sb", [P, 2, C])
        Wg_sb = sb("Wg_sb", [P, E0])
        W1_sb = sb("W1_sb", [P, E0, HID0])
        W2_sb = sb("W2_sb", [P, E0, HC, C])
        Wat_sb = sb("Wat_sb", [P, 4, C])
        rw1_sb = sb("rw1_sb", [P, RH])
        rw2_sb = sb("rw2_sb", [RH, E1])
        ew_sb = sb("ew_sb", [P, 3, E1, C])
        gb_b = sb("gb_b", [P, C])
        bo_b = sb("bo_b", [P, C])
        bg_b = sb("bg_b", [P, E0])
        rb2_b = sb("rb2_b", [P, E1])
        bias_rows = sb("bias_rows", [P, P])
        bias_T = sb("bias_T", [P, P])
        EB1, EB2, RB1 = E0 * HC, E0 * HC + E1, E0 * HC + 2 * E1
        b2_diag = sb("b2_diag", [TILES * EP, HTILES, C])
        b3_diag = sb("b3_diag", [TILES * EP, HTILES, C])
        ident = sb("ident", [P, P])
        identb = sb("identb", [P, P], BF16)
        countdown = sb("countdown", [P, NODES], F16)
        eidx = sb("eidx", [P, TILES, EP])
        zrows = sb("zrows", [1, C])
        pool_pad = sb("pool_pad", [1, 4])
        dve_pad = sb("dve_pad", [1, 4])

        xin = sb("xin", [P, TILES, C])
        xn0 = sb("xn0", [P, TILES, C])
        xn = sb("xn", [P, TILES, C])
        res = sb("res", [P, TILES, C])
        agg = sb("agg", [P, TILES, C])
        adj_sb = sb("adj_sb", [P, 2, NODES], I32)
        score = sb("score", [P, NODES], F16)
        top = sb("top", [P, TILES, TOP])
        slot_idx = sb("slot_idx", [P, TILES, SLOTS], U32)
        floor = sb("floor", [P, TILES])
        keep_next = sb("keep_next", [P, TILES])
        keep = sb("keep", [P, TILES])
        mask_next = sb("mask_next", [P, TILES, NODES], U8)
        mask = sb("mask", [P, TILES, NODES], BF16)
        G = sb("G", [P, 2, SLOTS, C])
        XT = sb("XT", [P, NODES])
        XT2 = sb("XT2", [P, NODES])
        st = sb("st", [P, TILES, 6])
        mv = sb("mv", [P, TILES, 2])
        sd = sb("sd", [P, TILES])
        sq = sb("sq", [P, TILES])
        rstd = sb("rstd", [P, TILES])
        lg = sb("lg", [P, TILES, EP])
        ex = sb("ex", [P, TILES, EP])
        pr_sb = sb("pr_sb", [P, TILES, EP])
        best = sb("best", [P, TILES, EP])
        besti = sb("besti", [P, TILES, EP], U32)
        bestf = sb("bestf", [P, TILES, EP])
        dlt = sb("dlt", [P, TILES])
        ed = sb("ed", [P, TILES])
        w1st = sb("w1st", [P, TILES])
        w2nd = sb("w2nd", [P, TILES])
        pick = sb("pick", [P, 2, TILES, EP])
        wts = sb("wts", [P, P // EP, EP])
        wtsP = wts[:, :, :].rearrange("p t e -> p (t e)")
        WT = sb("WT", [TILES * EP, P])
        tmp = sb("tmp", [P, HALF])
        HB = sb("HB", [P, 2, HC, HALF])
        QS = sb("QS", [P, HEADS, NODES], BF16)
        KS = sb("KS", [P, HEADS, NODES], BF16)
        VS = sb("VS", [P, TILES, HEADS, 32])
        rest = tmp
        MX = sb("MX", [P, HEADS, TILES])
        mrest = sb("mrest", [P, HEADS * TILES])
        mparts = sb("mparts", [P, PARTS, P], BF16)
        mT = sb("mT", [P, PARTS, P], BF16)
        CT = tmp
        rden = sb("rden", [P, HTILES, GH])
        ctxn = xn[:, 0:HTILES, :]
        XQ = HB[:, 0, 0:2, :].rearrange("p a (t c) -> p (a t) c", c=C)
        HBb = HB[:, :, :, :].rearrange("p a b c -> p (a b c)").bitcast(BF16)
        junk = HBb[:, 0:NODES]
        parts = HBb[:, 2 * NODES:].rearrange("p (s k n) -> p s k n", s=2, k=PARTS)
        PB = HB[:, :, :, :]

        PA = [ctx.enter_context(nc.psum_tensor(f"PA{i}", [P, NODES], F32)) for i in range(2)]
        PH = [ctx.enter_context(nc.psum_tensor(f"PH{i}", [P, HALF], F32)) for i in range(2)]
        PY = [ctx.enter_context(nc.psum_tensor("PY", [P, HALF], F32))]
        PM = [ctx.enter_context(nc.psum_tensor("PM", [P, HALF], F32))]
        BANK = {"A": PA, "H": PH, "Y": PY, "M": PM}
        full = {(n, i): sem(f"psum_{n}{i}_full") for n, r in BANK.items() for i in range(len(r))}
        free = {(n, i): sem(f"psum_{n}{i}_free") for n, r in BANK.items() for i in range(len(r))}

        def psum(key):
            n, i, _ = PLACE[key]
            return BANK[n][i]

        def wait_free(eng, key, b):
            n, i, j = PLACE[key]
            eng.wait_ge(free[n, i], b * USES[n] + (j + 1))

        def wait_full(eng, key, b):
            n, i, j = PLACE[key]
            eng.wait_ge(full[n, i], b * USES[n] + (j + 1))

        def wait_taken(eng, key, b):
            n, i, j = PLACE[key]
            eng.wait_ge(free[n, i], b * USES[n] + (j + 2))

        def filled(ins, key):
            n, i, _ = PLACE[key]
            ins.then_inc(full[n, i], 1)

        def emptied(ins, key):
            n, i, _ = PLACE[key]
            ins.then_inc(free[n, i], 1)

        s_w = sem("weights_loaded")
        s_const = sem("constants_made")
        s_ident = sem("identity_zeroed")
        s_btp = sem("bias_transposed")
        s_bt = sem("bias_columns_copied")
        s_xin = sem("x_loaded")
        s_adj = [sem(f"adjacency_loaded{i}") for i in range(2)]
        s_adjf = sem("adjacency_used")
        s_xn0 = sem("normed_input_ready")
        s_tab = sem("table_stored")
        s_idx = sem("slot_indices_ready")
        s_gat = [sem(f"neighbours_fetched{i}") for i in range(2)]
        s_gf = sem("neighbours_used")
        s_aggr = sem("aggregate_ready")
        s_x1 = sem("gnn_done")
        s_var = sem("variance_ready")
        s_sq = sem("deviation_ready")
        s_xn = sem("normed_ready")
        s_dl = sem("router_input_ready")
        s_ed = sem("router_exp_ready")
        s_wts = sem("expert_weights_ready")
        s_q1 = sem("first_part_ready")
        s_parts = sem("parts_ready")
        s_pd = sem("parts_stored")
        s_stack = sem("stacks_loaded")
        s_mp = sem("max_parts_ready")
        s_ms = sem("max_rows_stacked")
        s_out = sem("stored")
        W_LOADS = 0

        x_v = x.rearrange("b (t p) c -> b p t c", p=P)
        adj_v = adj.rearrange("b (t p) m -> b t p m", p=P)
        out_v = out.rearrange("b (t p) c -> b p t c", p=P)
        parts_v = parts_dram.rearrange("s k (h d) n -> s k d h n", d=D)
        block = ctx.enter_context(nc.Block())

        def held_by(eng, pad):
            if eng is nc.gpsimd or eng.engine == nc.gpsimd.engine:
                eng.tensor_tensor(pad[0:1, 0:1], pad[0:1, 1:2], pad[0:1, 2:3], ALU.add)
                eng.drain()
            else:
                eng.memset(pad[0:1, 0:1], 0.0)

        def over_graphs(eng, body):
            with eng.Fori(0, GRAPHS - 1) as b:
                body(b, True)
            body(GRAPHS - 1, False)

        loads = [
            (gW_sb[:, :, :], gW.rearrange("(k p) c -> p k c", p=P)), (Wg_sb[:, :], Wg),
            (W1_sb[:, :, :], W1.rearrange("e p h -> p e h")),
            (W2_sb[:, :, :, :], W2.rearrange("e (k p) c -> p e k c", p=P)),
            (Wat_sb[:, 0, :], Wq), (Wat_sb[:, 1, :], Wk), (Wat_sb[:, 2, :], Wv), (Wat_sb[:, 3, :], Wo),
            (rw1_sb[:, :], rw1), (rw2_sb[:, :], rw2),
            (ew_sb[:, 0, :, :], ew1.rearrange("e p h -> p e h")),
            (ew_sb[:, 1, :, :], ew2.rearrange("e p h -> p e h")),
            (ew_sb[:, 2, :, :], ew3.rearrange("e p h -> p e h")),
            (gb_b[:, :], gb.partition_broadcast(P)), (bo_b[:, :], bo.partition_broadcast(P)),
            (bg_b[:, :], bg.partition_broadcast(P)), (rb2_b[:, :], rb2.partition_broadcast(P)),
        ]
        late_loads = [
            (bias_rows[0:E0 * HC, :], b1.rearrange("e (k p) -> (e k) p", p=P)),
            (bias_rows[EB1:EB1 + E1, :], eb1), (bias_rows[EB2:EB2 + E1, :], eb2),
            (bias_rows[RB1:RB1 + 1, 0:RH], rb1.rearrange("(a n) -> a n", a=1)),
        ]
        for t in range(TILES):
            late_loads.append((b2_diag[t * EP:t * EP + E0, t % HTILES, :], b2))
            late_loads.append((b3_diag[t * EP:t * EP + E1, t % HTILES, :], eb3))
        N_LOADS = 16 * (len(loads) + len(late_loads))
        N_CONST = 8

        @block.sync
        def _(sp):
            def input_for(n):
                sp.dma_start(xin[:, :, :], x_v[n, :, :, :]).then_inc(s_xin, 16)

            def neighbours_for(n, after_first):
                sp.wait_ge(s_xn0, n + 1)
                sp.dma_start(table[0:NODES, :].rearrange("(t p) c -> p t c", p=P),
                             xn0[:, :, :]).then_inc(s_tab, 16)
                for t in range(TILES):
                    if after_first or t >= 2:
                        sp.wait_ge(s_adjf, n * TILES + (t - 1))
                    sp.dma_start(adj_sb[:, t % 2, :], adj_v[n, t, :, :]).then_inc(s_adj[t % 2], 16)

            input_for(0)
            for dst, src in loads:
                sp.dma_start(dst, src).then_inc(s_w, 16)
            sp.wait_ge(s_const, N_CONST)
            for dst, src in late_loads:
                sp.dma_start(dst, src).then_inc(s_w, 16)
            sp.dma_start(table[NODES:ROWS, :], zrows[:, :]).then_inc(s_out, 16)
            neighbours_for(0, False)

            def body(b, more):
                if more:
                    sp.wait_ge(s_x1, b + 1)
                    input_for(b + 1)
                    neighbours_for(b + 1, True)
                for i in range(2):
                    sp.wait_ge(s_parts, b * 2 + (i + 1))
                    sp.dma_start(parts_dram[i, :, :, :].rearrange("k p n -> p k n"),
                                 parts[:, i, :, :]).then_inc(s_pd, 16)
                for i, (stack, which) in enumerate(((QS, QPART), (KS, KPART))):
                    sp.wait_ge(s_pd, b * 32 + 32)
                    for j, k in enumerate(which):
                        sp.dma_start(stack[D * j:D * j + D, :, :],
                                     parts_v[i, k, :, :, :]).then_inc(s_stack, 16)
                wait_taken(sp, "mT", b)
                for k in range(PARTS):
                    sp.dma_start(QS[SROWS + k:SROWS + k + 1, :, :].rearrange("o h n -> o (h n)"),
                                 mT[0:HEADS * TILES, k, :]).then_inc(s_ms, 16)
                wait_taken(sp, ("y1", *ORDER1[-1]), b)
                sp.dma_start(out_v[b, :, :, :], res[:, :, :]).then_inc(s_out, 16)

            over_graphs(sp, body)
            sp.wait_ge(s_out, 16 * GRAPHS + 16)

        @block.gpsimd
        def _(pool):
            pool.memset(pool_pad[:, :], 0.0).then_inc(s_ident, 1)
            pool.memset(ident[:, :], 0.0).then_inc(s_ident, 1)
            pool.memset(identb[:, :], 0.0).then_inc(s_ident, 1)
            pool.memset(bias_rows[:, :], 0.0).then_inc(s_const, 1)
            pool.memset(b2_diag[:, :, :], 0.0).then_inc(s_const, 1)
            pool.memset(b3_diag[:, :, :], 0.0).then_inc(s_const, 1)
            pool.memset(zrows[:, :], 0.0).then_inc(s_const, 1)
            pool.iota(countdown[:, :], pattern=[[-1, NODES]], base=NODES, channel_multiplier=0,
                      allow_small_or_imprecise_dtypes=True).then_inc(s_const, 1)
            pool.iota(eidx[:, :, :], pattern=[[0, TILES], [1, EP]], base=0, channel_multiplier=0,
                      allow_small_or_imprecise_dtypes=True).then_inc(s_const, 1)
            pool.wait_ge(s_ident, 3)
            for m in (ident, identb):
                pool.affine_select(out=m[:, :], in_=m[:, :], compare_op=ALU.not_equal, fill=1.0,
                                   base=0, pattern=[[-1, P]], channel_multiplier=1).then_inc(s_const, 1)
            pool.wait_ge(s_const, N_CONST)
            pool.wait_ge(s_out, 16)

            def gathers(n):
                pool.wait_ge(s_tab, n * 16 + 16)
                for t in range(TILES):
                    pool.wait_ge(s_idx, n * TILES + (t + 1))
                    held_by(pool, pool_pad)
                    if t >= 2:
                        pool.wait_ge(s_gf, n * TILES + (t - 1))
                        held_by(pool, pool_pad)
                    for s in range(SLOTS):
                        pool.indirect_dma_start(
                            G[:, t % 2, s, :], None, table,
                            bass.IndirectOffsetOnAxis(slot_idx[:, t, s:s + 1], axis=0),
                            bounds_check=ROWS - 1, oob_is_err=False).then_inc(s_gat[t % 2], 16)

            gathers(0)
            with pool.Fori(1, GRAPHS) as n:
                gathers(n)

        @block.vector
        def _(dve):
            def settle(ins):
                dve.drain()
                return ins

            def norm(src, dst, n_norm, ready):
                for t in range(TILES):
                    dve.bn_stats(st[:, t, :], src[:, t, :])
                dve.drain()
                for t in range(TILES):
                    dve.bn_aggr(mv[:, t, :], st[:, t, :])
                dve.drain()
                settle(dve.tensor_scalar(sd[:, :], mv[:, :, 1], EPS, None, ALU.add).then_inc(s_var, 1))
                dve.wait_ge(s_sq, n_norm)
                settle(dve.reciprocal(rstd[:, :], sq[:, :]))
                for t in range(TILES):
                    last = dve.tensor_scalar(dst[:, t, :], src[:, t, :], mv[:, t, 0:1], rstd[:, t:t + 1],
                                             ALU.subtract, ALU.mult)
                if ready is not None:
                    last.then_inc(ready, 1)
                dve.drain()

            def norm_input(n, n_norm):
                dve.wait_ge(s_xin, n * 16 + 16)
                if isinstance(n, int) and n == 0:
                    pass
                else:
                    dve.wait_ge(s_tab, n * 16)
                norm(xin, xn0, n_norm, s_xn0)

            def find(n, t, rounds):
                if 0 in rounds:
                    dve.wait_ge(s_adj[t % 2], n * (16 * TILES // 2) + 16 * (t // 2 + 1))
                    settle(dve.scalar_tensor_tensor(out=score[:, :], in0=adj_sb[:, t % 2, :], scalar=0,
                                                    in1=countdown[:, :], op0=ALU.not_equal, op1=ALU.mult))
                for r in rounds:
                    settle(dve.max(top[:, t, 8 * r:8 * r + 8], score[:, :]))
                    if r == 0:
                        settle(dve.tensor_scalar(keep_next[:, t:t + 1], top[:, t, 0:1], 0.0, None, ALU.is_gt))
                        settle(dve.tensor_scalar(mask_next[:, t, :], adj_sb[:, t % 2, :], 0, keep_next[:, t:t + 1],
                                                 ALU.is_le, ALU.mult).then_inc(s_adjf, 1))
                    if r < ROUNDS - 1:
                        settle(dve.match_replace(score[:, :], top[:, t, 8 * r:8 * r + 8], score[:, :], 0.0))
                if ROUNDS - 1 in rounds:
                    settle(dve.tensor_scalar(slot_idx[:, t, :], top[:, t, 0:SLOTS], -1.0, float(NODES),
                                             ALU.mult, ALU.add).then_inc(s_idx, 1))
                    settle(dve.tensor_scalar(floor[:, t:t + 1], top[:, t, SLOTS:SLOTS + 1], 0.0, LOWEST,
                                             ALU.is_gt, ALU.mult))

            def pool_max(n, t):
                dve.wait_ge(s_gat[t % 2], n * (16 * SLOTS * TILES // 2) + 16 * SLOTS * (t // 2 + 1))
                settle(dve.tensor_reduce(out=agg[:, t, :], in_=G[:, t % 2, :, :].rearrange("p s c -> p c s"),
                                         axis=AX.X, op=ALU.max).then_inc(s_gf, 1))
                settle(dve.tensor_scalar(agg[:, t, :], agg[:, t, :], floor[:, t:t + 1], None,
                                         ALU.max).then_inc(s_aggr, 1))

            def gnn(b):
                for hf in range(2):
                    wait_full(dve, ("gnn", hf), b)
                    y = psum(("gnn", hf))[:, :].rearrange("p (t c) -> p t c", c=C)
                    tm = tmp[:, :].rearrange("p (t c) -> p t c", c=C)
                    tiles = slice(hf * HTILES, (hf + 1) * HTILES)
                    ins = dve.tensor_tensor(tm, y, gb_b[:, :].unsqueeze(1).to_broadcast([P, HTILES, C]), ALU.add)
                    emptied(ins, ("gnn", hf))
                    settle(ins)
                    ins = dve.scalar_tensor_tensor(out=res[:, tiles, :], in0=tm, scalar=0.0, in1=xin[:, tiles, :],
                                                   op0=ALU.max, op1=ALU.add)
                    if hf == 1:
                        ins.then_inc(s_x1, 1)
                    settle(ins)

            def choose(values, b, layer):
                for t in range(TILES):
                    dve.max(best[:, t, :], values[:, t, :])
                dve.drain()
                for t in range(TILES):
                    dve.max_index(besti[:, t, :], best[:, t, :], values[:, t, :])
                dve.drain()
                settle(dve.tensor_copy(bestf[:, :, 0:2], besti[:, :, 0:2]))
                settle(dve.tensor_tensor(dlt[:, :], best[:, :, 1], best[:, :, 0],
                                         ALU.subtract).then_inc(s_dl, 1))
                dve.wait_ge(s_ed, b * 3 + (1 if layer == 0 else 3))
                settle(dve.tensor_scalar(w1st[:, :], ed[:, :], 1.0, None, ALU.add))
                settle(dve.reciprocal(w1st[:, :], w1st[:, :]))
                settle(dve.tensor_tensor(w2nd[:, :], ed[:, :], w1st[:, :], ALU.mult))
                for i, w in enumerate((w1st, w2nd)):
                    settle(dve.tensor_tensor(pick[:, i, :, :], eidx[:, :, :],
                                             bestf[:, :, i:i + 1].to_broadcast([P, TILES, EP]), ALU.is_equal))
                    settle(dve.tensor_tensor(pick[:, i, :, :], pick[:, i, :, :],
                                             w[:, :].unsqueeze(2).to_broadcast([P, TILES, EP]), ALU.mult))
                settle(dve.tensor_tensor(wts[:, 0:TILES, :], pick[:, 0, :, :], pick[:, 1, :, :],
                                         ALU.add).then_inc(s_wts, 1))
                key = f"wT{layer}"
                wait_full(dve, key, b)
                ins = dve.tensor_copy(WT[:, :], psum(key)[0:TILES * EP, 0:P])
                emptied(ins, key)
                dve.drain()
                for hf in range(2):
                    key = (f"b{layer}", hf)
                    wait_full(dve, key, b)
                    tiles = slice(hf * HTILES, (hf + 1) * HTILES)
                    ins = dve.tensor_tensor(res[:, tiles, :], res[:, tiles, :],
                                            psum(key)[:, :].rearrange("p (t c) -> p t c", c=C), ALU.add)
                    emptied(ins, key)
                    settle(ins)

            def combine(b, layer, hf, e, last=False):
                key = (f"y{layer}", hf, e)
                wait_full(dve, key, b)
                for tt in range(HTILES):
                    t = hf * HTILES + tt
                    ins = dve.scalar_tensor_tensor(out=res[:, t, :], in0=psum(key)[:, tt * C:(tt + 1) * C],
                                                   scalar=wts[:, t, e:e + 1], in1=res[:, t, :],
                                                   op0=ALU.mult, op1=ALU.add)
                emptied(ins, key)
                dve.drain()
                return ins

            def split_parts(b, i, name):
                for hf in range(2):
                    cols = slice(hf * HALF, (hf + 1) * HALF)
                    wait_full(dve, (name, hf), b)
                    dve.wait_ge(s_q1, b * 4 + (2 * i + hf + 1))
                    ins = dve.tensor_tensor(rest[:, :], psum((name, hf))[:, :], parts[:, i, 0, cols], ALU.subtract)
                    emptied(ins, (name, hf))
                    settle(ins)
                    settle(dve.tensor_copy(parts[:, i, 1, cols], rest[:, :]))
                    ins = dve.tensor_tensor(parts[:, i, 2, cols], rest[:, :], parts[:, i, 1, cols], ALU.subtract)
                    if hf == 1:
                        ins.then_inc(s_parts, 1)
                    dve.drain()

            def attention(b, more):
                dve.drain()
                norm(res, xn, b * 4 + (4 if more else 3), None)
                for t in range(TILES):
                    last = dve.tensor_scalar(XQ[:, t, :], xn[:, t, :], keep[:, t:t + 1], None, ALU.mult)
                settle(last.then_inc(s_xn, 1))
                split_parts(b, 0, "q")
                split_parts(b, 1, "k")
                for t in range(TILES):
                    for h in range(HEADS):
                        key = ("s", t, h)
                        wait_full(dve, key, b)
                        held_by(dve, dve_pad)
                        ins = dve.tensor_tensor_reduce(out=junk[:, :], in0=psum(key)[:, :], in1=mask[:, t, :],
                                                       scale=1.0, scalar=LOWEST, op0=ALU.add, op1=ALU.max,
                                                       accum_out=MX[:, h, t:t + 1])
                        emptied(ins, key)
                        dve.drain()
                    if more and t >= 1:
                        pool_max(b + 1, t - 1)
                mx = MX[:, :, :].rearrange("p h t -> p (h t)")
                settle(dve.tensor_scalar(mrest[:, :], mx, -1.0, None, ALU.mult))
                for k in range(PARTS):
                    ins = dve.tensor_copy(mparts[:, k, 0:HEADS * TILES], mrest[:, :])
                    if k == PARTS - 1:
                        ins.then_inc(s_mp, 1)
                    dve.drain()
                    if k < PARTS - 1:
                        settle(dve.tensor_tensor(mrest[:, :], mrest[:, :], mparts[:, k, 0:HEADS * TILES],
                                                 ALU.subtract))
                wait_full(dve, "mT", b)
                ins = dve.tensor_copy(mT[:, :, :].rearrange("p k n -> p (k n)"),
                                      psum("mT")[:, :].bitcast(BF16)[:, 0:PARTS * P])
                emptied(ins, "mT")
                dve.drain()
                if more:
                    pool_max(b + 1, TILES - 1)
                for qh in range(2):
                    for g in range(2):
                        wait_full(dve, ("av", qh, g), b)
                        ins = dve.tensor_copy(CT[:, :], psum(("av", qh, g))[:, :])
                        emptied(ins, ("av", qh, g))
                        dve.drain()
                        key = ("ctx", qh, g)
                        wait_full(dve, key, b)
                        c4 = psum(key)[:, :].rearrange("p (q h d) -> p q h d", h=GH, d=32)
                        settle(dve.reciprocal(rden[:, :, :], c4[:, :, :, D]))
                        cn = ctxn[:, :, g * GH * D:(g + 1) * GH * D].rearrange("p q (h d) -> p q h d", d=D)
                        ins = dve.tensor_tensor(cn, c4[:, :, :, 0:D],
                                                rden[:, :, :].unsqueeze(3).to_broadcast([P, HTILES, GH, D]), ALU.mult)
                        emptied(ins, key)
                        dve.drain()
                    key = ("proj", qh)
                    wait_full(dve, key, b)
                    tiles = slice(qh * HTILES, (qh + 1) * HTILES)
                    y = psum(key)[:, :].rearrange("p (t c) -> p t c", c=C)
                    ins = dve.tensor_tensor(res[:, tiles, :], res[:, tiles, :], y, ALU.add)
                    emptied(ins, key)
                    settle(ins)
                    settle(dve.tensor_tensor(res[:, tiles, :], res[:, tiles, :],
                                             bo_b[:, :].unsqueeze(1).to_broadcast([P, HTILES, C]), ALU.add))

            dve.wait_ge(s_const, N_CONST)
            for bank in free.values():
                dve.memset(dve_pad[:, 0:1], 0.0).then_inc(bank, 1)
                dve.drain()
            dve.memset(VS[:, :, :, D:32], 0.0)
            dve.memset(KS[SROWS:SROWS + PARTS, :, :], 1.0)
            dve.memset(mparts[:, :, :], 0.0)
            dve.memset(wts[:, :, :], 0.0)
            dve.memset(lg[:, :, :], -1.0)
            dve.memset(pr_sb[:, :, :], -1.0)
            dve.drain()
            dve.memset(VS[:, :, :, D:D + 1], 1.0)
            dve.drain()
            dve.wait_ge(s_btp, 1)
            dve.tensor_copy(bias_T[:, :], PM[0][:, 0:P]).then_inc(s_bt, 1)
            dve.drain()
            norm_input(0, 1)
            for t in range(TILES):
                find(0, t, range(ROUNDS))
                if t >= 1:
                    pool_max(0, t - 1)
            pool_max(0, TILES - 1)

            def body(b, more):
                dve.wait_ge(s_out, b * 16 + 16)
                dve.tensor_scalar(mask[:, :, :], mask_next[:, :, :], -BIG, None, ALU.mult)
                dve.tensor_copy(keep[:, :], keep_next[:, :])
                dve.drain()
                gnn(b)
                norm(res, xn, b * 4 + 2, s_xn)
                wait_full(dve, "lg0", b)
                ins = dve.tensor_tensor(lg[:, :, 0:E0], psum("lg0")[:, 0:TILES * E0].rearrange("p (t e) -> p t e", e=E0),
                                        bg_b[:, :].unsqueeze(1).to_broadcast([P, TILES, E0]), ALU.add)
                emptied(ins, "lg0")
                settle(ins)
                choose(lg, b, 0)
                if more:
                    norm_input(b + 1, b * 4 + 3)
                for i, (hf, e) in enumerate(ORDER0):
                    if more:
                        find(b + 1, i // 2, range(2) if i % 2 == 0 else range(2, ROUNDS))
                    combine(b, 0, hf, e)
                attention(b, more)
                norm(res, xn, b * 4 + (5 if more else 4), s_xn)
                wait_full(dve, "lg1", b)
                ins = dve.tensor_tensor(lg[:, :, 0:E1], psum("lg1")[:, 0:TILES * E1].rearrange("p (t e) -> p t e", e=E1),
                                        rb2_b[:, :].unsqueeze(1).to_broadcast([P, TILES, E1]), ALU.add)
                emptied(ins, "lg1")
                settle(ins)
                settle(dve.tensor_reduce(out=dlt[:, :], in_=lg[:, :, 0:E1], axis=AX.X, op=ALU.max))
                settle(dve.tensor_tensor(lg[:, :, 0:E1], lg[:, :, 0:E1],
                                         dlt[:, :].unsqueeze(2).to_broadcast([P, TILES, E1]),
                                         ALU.subtract).then_inc(s_dl, 1))
                dve.wait_ge(s_ed, b * 3 + 2)
                settle(dve.tensor_reduce(out=dlt[:, :], in_=ex[:, :, 0:E1], axis=AX.X, op=ALU.add))
                settle(dve.reciprocal(dlt[:, :], dlt[:, :]))
                settle(dve.tensor_tensor(pr_sb[:, :, 0:E1], ex[:, :, 0:E1],
                                         dlt[:, :].unsqueeze(2).to_broadcast([P, TILES, E1]), ALU.mult))
                choose(pr_sb, b, 1)
                for hf, e in ORDER1:
                    last = combine(b, 1, hf, e)

            over_graphs(dve, body)

        @block.scalar
        def _(act):
            def root(n):
                act.wait_ge(s_var, n)
                act.activation(sq[:, :], sd[:, :], ACT.Sqrt).then_inc(s_sq, 1)

            def copy_out(dst, key, b):
                wait_full(act, key, b)
                emptied(act.activation(dst, psum(key)[:, :], ACT.Copy), key)

            root(1)

            def body(b, more):
                H = lambda hf: slice(hf * HALF, (hf + 1) * HALF)
                for hf in range(2):
                    copy_out(XT[:, H(hf)], ("xn", hf), b)
                    copy_out(XT2[:, H(hf)], ("agg", hf), b)
                root(b * 4 + 2)
                for hf in range(2):
                    copy_out(XT[:, H(hf)], ("t0", hf), b)
                act.wait_ge(s_dl, b * 3 + 1)
                act.activation(ed[:, :], dlt[:, :], ACT.Exp).then_inc(s_ed, 1)
                if more:
                    root(b * 4 + 3)
                for i, (hf, e) in enumerate(ORDER0):
                    for c in range(HC):
                        key = ("h0", hf, e, c)
                        wait_full(act, key, b)
                        ins = act.activation(HB[:, i % 2, c, :], psum(key)[:, :], ACT.Gelu,
                                             bias=bias_T[:, e * HC + c:e * HC + c + 1])
                        emptied(ins, key)
                root(b * 4 + (4 if more else 3))
                for hf in range(2):
                    copy_out(XT[:, H(hf)], ("ta", hf), b)
                for hf in range(2):
                    copy_out(XT2[:, H(hf)], ("tq", hf), b)
                for i, name in enumerate(("q", "k")):
                    for hf in range(2):
                        wait_full(act, (name, hf), b)
                        act.activation(parts[:, i, 0, H(hf)], psum((name, hf))[:, :], ACT.Copy).then_inc(s_q1, 1)
                for hf in range(2):
                    key = ("v", hf)
                    wait_full(act, key, b)
                    ins = act.activation(VS[:, hf * HTILES:(hf + 1) * HTILES, :, 0:D],
                                   psum(key)[:, :].rearrange("p (t h d) -> p t h d", h=HEADS, d=D),
                                   ACT.Copy)
                    emptied(ins, key)
                n = 0
                for qh in range(2):
                    for g in range(2):
                        for kc in range(TILES):
                            for pr in range(2):
                                key = ("st", qh, g, kc, pr)
                                wait_full(act, key, b)
                                ins = act.activation(PB[:, kc % 2, 2 * pr:2 * pr + 2, :],
                                                     psum(key)[:, :].rearrange("p (h q) -> p h q", h=2),
                                                     ACT.Exp, scale=float(D) ** -0.5)
                                emptied(ins, key)
                    copy_out(XT[:, H(qh)], ("ctxT", qh), b)
                root(b * 4 + (5 if more else 4))
                for hf in range(2):
                    copy_out(XT[:, H(hf)], ("t1", hf), b)
                for hf in range(2):
                    key = ("r1", hf)
                    wait_full(act, key, b)
                    emptied(act.activation(XT2[0:RH, H(hf)], psum(key)[0:RH, :], ACT.Relu,
                                           bias=bias_T[0:RH, RB1:RB1 + 1]), key)
                act.wait_ge(s_dl, b * 3 + 2)
                act.activation(ex[:, :, 0:E1], lg[:, :, 0:E1], ACT.Exp).then_inc(s_ed, 1)
                act.wait_ge(s_dl, b * 3 + 3)
                act.activation(ed[:, :], dlt[:, :], ACT.Exp).then_inc(s_ed, 1)
                for i in range(len(ORDER1) + 1):
                    for name, j, col in (("u1", i, EB1), ("u2", i - 1, EB2)):
                        if 0 <= j < len(ORDER1):
                            hf, e = ORDER1[j]
                            key = (name, hf, e)
                            wait_full(act, key, b)
                            k = 0 if name == "u1" else 2
                            ins = act.activation(HB[:, 0, k + j % 2, :], psum(key)[:, :], ACT.Relu,
                                                 bias=bias_T[:, col + e:col + e + 1])
                            emptied(ins, key)

            over_graphs(act, body)

        @block.tensor
        def _(pe):
            def transposes(key, src, hf, b):
                wait_free(pe, key, b)
                for tt in range(HTILES):
                    ins = pe.transpose(psum(key)[:, tt * P:(tt + 1) * P], src[:, hf * HTILES + tt, :], ident[:, :])
                filled(ins, key)

            pe.wait_ge(s_w, N_LOADS)
            pe.wait_ge(s_const, N_CONST)
            pe.transpose(PM[0][:, 0:P], bias_rows[:, :], ident[:, :]).then_inc(s_btp, 1)
            pe.wait_ge(s_bt, 1)

            def body(b, more):
                pe.wait_ge(s_xn0, b + 1)
                pe.wait_ge(s_aggr, b * TILES + TILES)
                for hf in range(2):
                    transposes(("xn", hf), xn0, hf, b)
                    transposes(("agg", hf), agg, hf, b)
                    wait_taken(pe, ("xn", hf), b)
                    wait_taken(pe, ("agg", hf), b)
                    key = ("gnn", hf)
                    wait_free(pe, key, b)
                    for tt in range(HTILES):
                        t = hf * HTILES + tt
                        o = psum(key)[:, tt * C:(tt + 1) * C]
                        pe.matmul(o, XT[:, t * P:(t + 1) * P], gW_sb[:, 0, :], start=True, stop=False)
                        ins = pe.matmul(o, XT2[:, t * P:(t + 1) * P], gW_sb[:, 1, :], start=False, stop=True)
                    filled(ins, key)
                pe.wait_ge(s_xn, b * 3 + 1)
                for hf in range(2):
                    transposes(("t0", hf), xn, hf, b)
                wait_taken(pe, ("t0", 0), b)
                wait_taken(pe, ("t0", 1), b)
                wait_free(pe, "lg0", b)
                for t in range(TILES):
                    ins = pe.matmul(psum("lg0")[:, t * E0:(t + 1) * E0], XT[:, t * P:(t + 1) * P], Wg_sb[:, :],
                                    start=True, stop=True)
                filled(ins, "lg0")

                def expert_bias(layer, diag):
                    pe.wait_ge(s_wts, b * 2 + (layer + 1))
                    key = f"wT{layer}"
                    wait_free(pe, key, b)
                    filled(pe.transpose(psum(key)[:, 0:P], wtsP, ident[:, :]), key)
                    wait_taken(pe, key, b)
                    for hf in range(2):
                        key = (f"b{layer}", hf)
                        wait_free(pe, key, b)
                        rows = slice(hf * HTILES * EP, (hf + 1) * HTILES * EP)
                        filled(pe.matmul(psum(key)[:, :], WT[rows, :],
                                         diag[rows, :, :].rearrange("k t c -> k (t c)"),
                                         start=True, stop=True), key)

                expert_bias(0, b2_diag)

                def up0(i):
                    hf, e = ORDER0[i]
                    for c in range(HC):
                        key = ("h0", hf, e, c)
                        wait_free(pe, key, b)
                        filled(pe.matmul(psum(key)[:, :], W1_sb[:, e, c * P:(c + 1) * P],
                                         XT[:, hf * HALF:(hf + 1) * HALF], start=True, stop=True), key)

                def down0(i):
                    hf, e = ORDER0[i]
                    key = ("y0", hf, e)
                    for c in (HC - 2, HC - 1):
                        wait_taken(pe, ("h0", hf, e, c), b)
                    wait_free(pe, key, b)
                    for tt in range(HTILES):
                        for c in range(HC):
                            ins = pe.matmul(psum(key)[:, tt * C:(tt + 1) * C],
                                            HB[:, i % 2, c, tt * P:(tt + 1) * P], W2_sb[:, e, c, :],
                                            start=(c == 0), stop=(c == HC - 1))
                    filled(ins, key)

                for i in range(len(ORDER0) + 1):
                    if i < len(ORDER0):
                        up0(i)
                    if i >= 1:
                        down0(i - 1)

                pe.wait_ge(s_xn, b * 3 + 2)
                for hf in range(2):
                    transposes(("ta", hf), xn, hf, b)
                for hf in range(2):
                    transposes(("tq", hf), XQ, hf, b)
                for hf in range(2):
                    wait_taken(pe, ("ta", hf), b)
                    wait_taken(pe, ("tq", hf), b)
                for i, name, src in ((0, "q", XT2), (1, "k", XT)):
                    for hf in range(2):
                        key = (name, hf)
                        wait_free(pe, key, b)
                        filled(pe.matmul(psum(key)[:, :], Wat_sb[:, i, :], src[:, hf * HALF:(hf + 1) * HALF],
                                         start=True, stop=True), key)
                for hf in range(2):
                    key = ("v", hf)
                    wait_free(pe, key, b)
                    for tt in range(HTILES):
                        t = hf * HTILES + tt
                        ins = pe.matmul(psum(key)[:, tt * C:(tt + 1) * C], XT[:, t * P:(t + 1) * P],
                                        Wat_sb[:, 2, :], start=True, stop=True)
                    filled(ins, key)
                pe.wait_ge(s_stack, (b + 1) * (16 * 2 * PAIRS))
                for t in range(TILES):
                    for h in range(HEADS):
                        key = ("s", t, h)
                        wait_free(pe, key, b)
                        for hf in range(2):
                            ins = pe.matmul(psum(key)[:, hf * HALF:(hf + 1) * HALF],
                                            QS[0:SROWS, h, t * P:(t + 1) * P],
                                            KS[0:SROWS, h, hf * HALF:(hf + 1) * HALF], start=True, stop=True)
                        filled(ins, key)
                pe.wait_ge(s_mp, b + 1)
                wait_free(pe, "mT", b)
                for k in range(PARTS):
                    ins = pe.transpose(psum("mT")[:, :].bitcast(BF16)[:, k * P:(k + 1) * P], mparts[:, k, :],
                                       identb[:, :])
                filled(ins, "mT")
                pe.wait_ge(s_ms, (b + 1) * (16 * PARTS))
                wait_taken(pe, ("v", 0), b)
                wait_taken(pe, ("v", 1), b)

                def scores(qh, g, kc):
                    for pr in range(2):
                        key = ("st", qh, g, kc, pr)
                        wait_free(pe, key, b)
                        for hh in range(2):
                            h = g * GH + 2 * pr + hh
                            o = psum(key)[:, hh * HALF:(hh + 1) * HALF]
                            pe.matmul(o, KS[0:SROWS + PARTS, h, kc * P:(kc + 1) * P],
                                      QS[0:SROWS + PARTS, h, qh * HALF:(qh + 1) * HALF], start=True, stop=False)
                            for qt in range(HTILES):
                                ins = pe.matmul(o[:, qt * P:(qt + 1) * P],
                                                mask[:, qh * HTILES + qt, kc * P:(kc + 1) * P], identb[:, :],
                                                start=False, stop=(qt == HTILES - 1))
                        filled(ins, key)

                def context(qh, g, kc):
                    for pr in range(2):
                        wait_taken(pe, ("st", qh, g, kc, pr), b)
                    key = ("av", qh, g)
                    if kc == 0:
                        wait_free(pe, key, b)
                    for hh in range(GH):
                        ins = pe.matmul(psum(key)[32 * hh:32 * hh + 32, :], VS[:, kc, g * GH + hh, :],
                                        PB[:, kc % 2, hh, :], start=(kc == 0), stop=(kc == TILES - 1))
                    if kc == TILES - 1:
                        filled(ins, key)

                for qh in range(2):
                    for g in range(2):
                        scores(qh, g, 0)
                        for kc in range(TILES):
                            if kc + 1 < TILES:
                                scores(qh, g, kc + 1)
                            context(qh, g, kc)
                        wait_taken(pe, ("av", qh, g), b)
                        key = ("ctx", qh, g)
                        wait_free(pe, key, b)
                        for tt in range(HTILES):
                            ins = pe.transpose(psum(key)[:, tt * P:(tt + 1) * P], CT[:, tt * P:(tt + 1) * P],
                                               ident[:, :])
                        filled(ins, key)
                    wait_taken(pe, ("ctx", qh, 0), b)
                    wait_taken(pe, ("ctx", qh, 1), b)
                    transposes(("ctxT", qh), ctxn, 0, b)
                    wait_taken(pe, ("ctxT", qh), b)
                    key = ("proj", qh)
                    wait_free(pe, key, b)
                    for tt in range(HTILES):
                        t = qh * HTILES + tt
                        ins = pe.matmul(psum(key)[:, tt * C:(tt + 1) * C], XT[:, t * P:(t + 1) * P],
                                        Wat_sb[:, 3, :], start=True, stop=True)
                    filled(ins, key)

                pe.wait_ge(s_xn, b * 3 + 3)
                for hf in range(2):
                    transposes(("t1", hf), xn, hf, b)
                wait_taken(pe, ("t1", 0), b)
                wait_taken(pe, ("t1", 1), b)
                for hf in range(2):
                    key = ("r1", hf)
                    wait_free(pe, key, b)
                    filled(pe.matmul(psum(key)[0:RH, :], rw1_sb[:, :], XT[:, hf * HALF:(hf + 1) * HALF],
                                     start=True, stop=True), key)
                wait_taken(pe, ("r1", 0), b)
                wait_taken(pe, ("r1", 1), b)
                wait_free(pe, "lg1", b)
                for t in range(TILES):
                    ins = pe.matmul(psum("lg1")[:, t * E1:(t + 1) * E1], XT2[0:RH, t * P:(t + 1) * P],
                                    rw2_sb[:, :], start=True, stop=True)
                filled(ins, "lg1")
                expert_bias(1, b3_diag)
                n1 = len(ORDER1)

                for i in range(n1 + 2):
                    if i < n1:
                        hf, e = ORDER1[i]
                        key = ("u1", hf, e)
                        wait_free(pe, key, b)
                        filled(pe.matmul(psum(key)[:, :], ew_sb[:, 0, e, :], XT[:, hf * HALF:(hf + 1) * HALF],
                                         start=True, stop=True), key)
                    if 1 <= i <= n1:
                        j = i - 1
                        hf, e = ORDER1[j]
                        key = ("u2", hf, e)
                        wait_taken(pe, ("u1", hf, e), b)
                        wait_free(pe, key, b)
                        filled(pe.matmul(psum(key)[:, :], ew_sb[:, 1, e, :], HB[:, 0, j % 2, :],
                                         start=True, stop=True), key)
                    if i >= 2:
                        j = i - 2
                        hf, e = ORDER1[j]
                        key = ("y1", hf, e)
                        wait_taken(pe, ("u2", hf, e), b)
                        wait_free(pe, key, b)
                        for tt in range(HTILES):
                            ins = pe.matmul(psum(key)[:, tt * C:(tt + 1) * C], HB[:, 0, 2 + j % 2, tt * P:(tt + 1) * P],
                                            ew_sb[:, 2, e, :], start=True, stop=True)
                        filled(ins, key)

            over_graphs(pe, body)


_INS = ['x', 'adj', 'L0_gnn_W', 'L0_gnn_b', 'L0_ffn_Wg', 'L0_ffn_bg', 'L0_ffn_W1', 'L0_ffn_b1', 'L0_ffn_W2',
        'L0_ffn_b2', 'L1_gnn_Wq', 'L1_gnn_Wk', 'L1_gnn_Wv', 'L1_gnn_Wo', 'L1_gnn_bo', 'L1_ffn_router_w1',
        'L1_ffn_router_b1', 'L1_ffn_router_w2', 'L1_ffn_router_b2', 'L1_ffn_expert_w1', 'L1_ffn_expert_b1',
        'L1_ffn_expert_w2', 'L1_ffn_expert_b2', 'L1_ffn_expert_w3', 'L1_ffn_expert_b3']


def kernel(**inputs):
    import numpy as np
    import concourse.bacc as bacc
    from concourse.bass_utils import run_bass_kernel_spmd

    nc = bacc.Bacc("TRN2", target_bir_lowering=False, num_devices=1)
    arrays, args = {}, []
    for name in _INS:
        a = np.ascontiguousarray(inputs[name])
        arrays[f"in_{name}"] = a
        args.append(nc.dram_tensor(f"in_{name}", a.shape, mybir.dt.from_np(a.dtype), kind="ExternalInput").ap())
    out = nc.dram_tensor("out_x", (GRAPHS, NODES, C), F32, kind="ExternalOutput").ap()
    graph_kernel(nc, *args, out)
    r = run_bass_kernel_spmd(nc, [arrays], core_ids=[0])
    return r.results[0]["out_x"]
```

```python
from contextlib import ExitStack

import concourse.bass as bass
from concourse import mybir

F32 = mybir.dt.float32
BF16 = mybir.dt.bfloat16
F16 = mybir.dt.float16
U8 = mybir.dt.uint8
I32 = mybir.dt.int32
U32 = mybir.dt.uint32
ALU = mybir.AluOpType
ACT = mybir.ActivationFunctionType
AX = mybir.AxisListType

GRAPHS, NODES, C = 8, 1024, 128
P = 128
TILES = NODES // P
HALF = 512
HTILES = HALF // P
SLOTS = 25
TOP = 32
ROUNDS = TOP // 8
ROWS = NODES + 1
E0, HID0 = 8, 512
HC = HID0 // P
E1, RH = 6, 64
EP = 8
HEADS, D = 8, 16
PARTS = 3
PAIRS = 6
QPART = [0, 1, 0, 1, 2, 0]
KPART = [0, 0, 1, 1, 0, 2]
SROWS = PAIRS * D
GH = 4
BIG = float(2 ** 30)
LOWEST = -3.0e38
EPS = 1e-5


ORDER0 = [(hf, e) for hf in range(2) for e in range(E0)]
ORDER1 = [(hf, e) for hf in range(2) for e in range(E1)]


def schedule(back, front, near):
    s = []
    finds = [("find", t, r) for t in range(TILES) for r in range(2)] if near else []
    pools = [("pmax", t) for t in range(TILES)] if near else []
    units = list(range(len(ORDER0))) if front else []
    scores = [("s", t, h) for t in range(TILES) for h in range(HEADS)] if back else []

    def find(n=1):
        for _ in range(min(n, len(finds))):
            f = finds.pop(0)
            s.append(f)
            if f[2] == 1 and f[1] + 2 < TILES:
                s.append(("load_adj", f[1] + 2))

    def pool():
        if pools:
            s.append(pools.pop(0))

    def score(n):
        for _ in range(min(n, len(scores))):
            k = scores.pop(0)
            if k[2] == 0:
                s.append(("mask", k[1]))
            s.append(k)
            if k[2] == 0 and k[1] + 1 < TILES:
                s.append(("load_mask", k[1] + 1))

    def run_units(count, each_score=0, each_find=0):
        mine = [units.pop(0) for _ in range(min(count, len(units)))]
        for k in range(len(mine) + 1):
            left = each_score
            for c in range(HC):
                if k < len(mine):
                    s.append(("up0", mine[k], c))
                if k > 0 and c % 2 == 1 and left > 0:
                    score(min(2, left))
                    left -= 2
            if k > 0:
                for tt in range(HTILES):
                    s.append(("down0", mine[k - 1], tt))
                    if left > 0:
                        score(1)
                        left -= 1
                s.append(("acc0", mine[k - 1]))
                score(left)
                find(each_find)

    if back:
        s += [("load_mask", 0), ("take",)]
    if front:
        s += [("load_res",), ("gnn",)]
    if back:
        s += [("ln", 2), ("qT",)]
    if front:
        s.append(("gnn_add",))
    if near:
        s += [("load_x",)]
    if back:
        s.append(("qk", 0))
    if front:
        s.append(("ln", 1))
    if back:
        s += [("qk", 1), ("v",)]
    if front:
        s += [("t0",), ("choose", 0)]
    if near:
        s += [("ln", 0), ("store_x",), ("load_adj", 0), ("load_adj", 1)]
    if back:
        run_units(3, 0, 2)
        for n in range(3):
            run_units(3 if n < 2 else 4, 6 if front else 64, 1)
            pool()
        score(len(scores))
        s.append(("mparts",))
        run_units(1, 0, 1)
        s.append(("mT",))
        find(len(finds))
        groups = [(qh, g) for qh in range(2) for g in range(2)]
        for n, (qh, g) in enumerate(groups):
            for kc in range(TILES):
                s.append(("st", qh, g, kc))
                if kc == 1 and n > 0:
                    s.append(("fin", *groups[n - 1]))
                if kc == 3 and n == 2:
                    s.append(("proj", 0))
                if kc > 0:
                    s.append(("av", qh, g, kc - 1))
                if kc == 5:
                    pool()
            s.append(("av", qh, g, TILES - 1))
        s += [("fin", 1, 1), ("proj", 1)]
        s.append(("ln", 3))
        run_units(len(units))
        s += [("t1",), ("choose", 1)]
        n1 = len(ORDER1)
        for k in range(n1 + 3):
            if k < n1:
                s.append(("u1", k))
            if 1 <= k <= n1:
                s.append(("u2", k - 1))
            if 2 <= k <= n1 + 1:
                s.append(("y1", k - 2))
            if k >= 3:
                s.append(("acc1", k - 3))
        while pools:
            pool()
        s.append(("store",))
    elif not front:
        for t in range(TILES):
            find(2)
            if t > 0:
                pool()
        pool()
    else:
        run_units(8, 0, 2)
        while pools:
            run_units(2)
            pool()
        run_units(len(units))
    return s


def signals(step):
    k = step[0]
    H = lambda *key: [("H", key, 1)]
    if k == "ln":
        return [("var", step, 1), ("sq", step, 1), ("xn0" if step[1] == 0 else "xn", step, 1)]
    if k == "gnn":
        return sum([H("xn", hf) + H("agg", hf) + [("YM"[hf], ("gnn", hf), 1)] for hf in range(2)], [])
    if k == "gnn_add":
        return [("x1", step, 1)]
    if k == "take":
        return [("took", step, 1)]
    if k == "load_res":
        return [("resx", step, 16)]
    if k == "load_x":
        return [("xin", step, 16)]
    if k == "store_x":
        return [("tab", step, 16)]
    if k == "load_adj":
        return [(f"adj{step[1] % 2}", step, 16)]
    if k == "load_mask":
        return [("adjm", step, 16)]
    if k == "mask":
        return [("adjmf", step, 1)]
    if k == "find":
        return [("adjf", step, 1)] if step[2] == 0 else [("idx", step, 1)]
    if k == "pmax":
        return [(f"gat{step[1] % 2}", step, 16 * SLOTS), ("gf", step, 1), ("aggr", step, 1)]
    if k == "qT":
        return H("ta", 0) + H("ta", 1) + H("tq", 0) + H("tq", 1)
    if k == "qk":
        i = step[1]
        return (H("qk", i, 0) + H("qk", i, 1) + [("q1", ("q1", i, 0), 1), ("q1", ("q1", i, 1), 1),
                ("parts", step, 1), ("pd", step, 16), ("stack", step, 16 * PAIRS)])
    if k == "v":
        return H("v", 0) + H("v", 1)
    if k == "t0":
        return H("t0", 0) + H("t0", 1) + [("M", "lg0", 1)]
    if k == "t1":
        return H("t1", 0) + H("t1", 1) + H("r1", 0) + H("r1", 1) + [("M", "lg1", 1)]
    if k == "choose":
        i = step[1]
        return ([("dl", ("sm",), 1), ("ed", ("sm",), 1)] if i == 1 else []) + [
            ("dl", step, 1), ("ed", step, 1), ("wts", step, 1), ("M", f"wT{i}", 1)] + H("b", i, 0) + H("b", i, 1)
    if k == "up0":
        return H(*step)
    if k == "down0":
        return [("Y", ("y0", step[1]), 1)] if step[2] == HTILES - 1 else []
    if k == "s":
        return [("A", step, 1)]
    if k == "mparts":
        return [("mp", step, 1)]
    if k == "mT":
        return [("M", "mT", 1), ("ms", step, 16 * PARTS)]
    if k == "st":
        return [("A", (*step, pr), 1) for pr in range(2)]
    if k == "av":
        return [("Y", ("av", step[1], step[2]), 1)] if step[3] == TILES - 1 else []
    if k == "fin":
        return H("ctx", step[1], step[2])
    if k == "proj":
        return H("ctxT", step[1]) + H("proj", step[1])
    if k in ("u1", "u2"):
        return H(*step)
    if k == "y1":
        return [("Y", step, 1)]
    if k == "store":
        return [("out", step, 16)]
    return []


BANKS = {"A": 2, "H": 2, "Y": 1, "M": 1}


class Pass:

    def __init__(self, before, back, front, near):
        self.back, self.front, self.near = back, front, near
        self.steps = schedule(back, front, near)
        self.start = dict(before)
        self.place, self.bank, ring = {}, {}, dict(before.get("ring", {}))
        count = {}
        for step in self.steps:
            for name, key, much in signals(step):
                if name in BANKS:
                    n = ring.get(name, 0)
                    ring[name] = n + 1
                    self.bank[key] = (name, n % BANKS[name])
                    name = f"{name}{n % BANKS[name]}"
                count[name] = count.get(name, 0) + much
                self.place[key if not isinstance(key, tuple) or key[0] not in KEYED else (name, key)] = (name, count[name])
        self.count = count
        self.ring = ring

    def after(self, times):
        if times > 1:
            assert all((self.ring[n] - self.start["ring"].get(n, 0)) % BANKS[n] == 0 for n in self.ring)
        end = {n: self.start.get(n, 0) + times * c for n, c in self.count.items()}
        return {**self.start, **end, "ring": self.ring}


KEYED = ("ln", "pmax", "qk", "choose", "sm", "find", "mT")


def graph_kernel(nc, x, adj, gW, gb, Wg, bg, W1, b1, W2, b2, Wq, Wk, Wv, Wo, bo,
                 rw1, rb1, rw2, rb2, ew1, eb1, ew2, eb2, ew3, eb3, out):
    ctx = ExitStack()
    with ctx:
        def sb(name, shape, dt=F32):
            return ctx.enter_context(nc.sbuf_tensor(name, shape, dt))

        def sem(name):
            return ctx.enter_context(nc.semaphore(name))

        table = nc.dram_tensor("table", (ROWS, C), F32, kind="Internal").ap()
        parts_dram = nc.dram_tensor("parts_dram", (2, PARTS, P, NODES), BF16, kind="Internal").ap()

        gW_sb = sb("gW_sb", [P, 2, C])
        Wg_sb = sb("Wg_sb", [P, E0])
        W1_sb = sb("W1_sb", [P, E0, HID0])
        W2_sb = sb("W2_sb", [P, E0, HC, C])
        Wat_sb = sb("Wat_sb", [P, 4, C])
        rw1_sb = sb("rw1_sb", [P, RH])
        rw2_sb = sb("rw2_sb", [RH, E1])
        ew_sb = sb("ew_sb", [P, 3, E1, C])
        gb_b = sb("gb_b", [P, C])
        bo_b = sb("bo_b", [P, C])
        bg_b = sb("bg_b", [P, E0])
        rb2_b = sb("rb2_b", [P, E1])
        bias_T = sb("bias_T", [P, P])
        EB1, EB2, RB1 = E0 * HC, E0 * HC + E1, E0 * HC + 2 * E1
        bias_diag = sb("bias_diag", [2 * TILES * EP, HTILES, C])
        ident = sb("ident", [P, P])
        identb = sb("identb", [P, P], BF16)
        countdown = sb("countdown", [P, NODES], F16)
        eidx = sb("eidx", [P, TILES, EP])
        pool_pad = sb("pool_pad", [1, 4])
        dve_pad = sb("dve_pad", [1, 4])

        xn0 = sb("xn0", [P, TILES, C])
        adj_sb = sb("adj_sb", [P, 2, NODES], I32)
        score = sb("score", [P, NODES], F16)
        top = sb("top", [P, 2, TOP])
        slot_idx = sb("slot_idx", [P, TILES, SLOTS], U32)
        floor = sb("floor", [P, TILES])
        keeps = [sb(f"keep{i}", [P, TILES]) for i in range(3)]
        G = sb("G", [P, 2, SLOTS, C])
        agg = sb("agg", [P, TILES, C])
        res_b = sb("res_b", [P, TILES, C])
        res_n = sb("res_n", [P, TILES, C])
        xn = sb("xn", [P, TILES, C])
        XT = sb("XT", [P, NODES])
        XT2 = sb("XT2", [P, NODES])
        XB = sb("XB", [P, NODES])
        st = sb("st", [P, TILES, 6])
        mv = sb("mv", [P, TILES, 2])
        sd = sb("sd", [P, TILES])
        sq = sb("sq", [P, TILES])
        rstd = sb("rstd", [P, TILES])
        lg = sb("lg", [P, TILES, EP])
        ex = sb("ex", [P, TILES, EP])
        pr_sb = sb("pr_sb", [P, TILES, EP])
        best = sb("best", [P, TILES, EP])
        besti = sb("besti", [P, TILES, EP], U32)
        bestf = sb("bestf", [P, TILES, EP])
        dlt = sb("dlt", [P, TILES])
        ed = sb("ed", [P, TILES])
        w1st = sb("w1st", [P, TILES])
        w2nd = sb("w2nd", [P, TILES])
        pick = sb("pick", [P, 2, TILES, EP])
        wts = [sb(f"wts{i}", [P, P // EP, EP]) for i in range(2)]
        WT = sb("WT", [2 * TILES * EP, P])
        tmp = sb("tmp", [P, HALF])
        bias_rows = tmp[:, 0:P]
        zrows = tmp[0:1, P:2 * P]
        HB = sb("HB", [P, 2, HC, HALF])
        adjm = sb("adjm", [P, NODES], I32)
        drop = sb("drop", [P, TILES])
        mask = sb("mask", [P, TILES, NODES], BF16)
        QS = sb("QS", [P, HEADS, NODES], BF16)
        KS = sb("KS", [P, HEADS, NODES], BF16)
        VS = sb("VS", [P, TILES, HEADS * (D + 1) + 32 - (D + 1)])
        VH = VS[:, :, 0:HEADS * (D + 1)].rearrange("p t (h e) -> p t h e", e=D + 1)
        parts = sb("parts", [P, PARTS, NODES], BF16)
        junk = parts[:, 0, :]
        MX = sb("MX", [P, HEADS, TILES])
        mrest = sb("mrest", [P, HEADS * TILES])
        mparts = sb("mparts", [P, PARTS, P], BF16)
        mT = sb("mT", [P, PARTS, P], BF16)
        rden = sb("rden", [P, HTILES, GH])
        XQ = HB[:, 0, 0:2, :].rearrange("p a (t c) -> p (a t) c", c=C)
        rest = tmp
        CT = tmp
        ctxn = xn[:, 0:HTILES, :]

        ring_banks = {
            "A": [ctx.enter_context(nc.psum_tensor(f"PA{i}", [P, NODES], F32)) for i in range(2)],
            "H": [ctx.enter_context(nc.psum_tensor(f"PH{i}", [P, HALF], F32)) for i in range(2)],
            "Y": [ctx.enter_context(nc.psum_tensor("PY", [P, HALF], F32))],
            "M": [ctx.enter_context(nc.psum_tensor("PM", [P, HALF], F32))],
        }
        full = {f"{n}{i}": sem(f"psum_{n}{i}_full") for n, r in ring_banks.items() for i in range(len(r))}
        free = {f"{n}{i}": sem(f"psum_{n}{i}_free") for n, r in ring_banks.items() for i in range(len(r))}

        s_w = sem("weights_loaded")
        s_const = sem("constants_made")
        s_ident = sem("identity_zeroed")
        s_btp = sem("bias_transposed")
        s_bt = sem("bias_columns_copied")
        S = {name: sem(words) for name, words in {
            "var": "variance_ready", "sq": "deviation_ready", "xn0": "normed_input_ready",
            "xn": "normed_ready", "x1": "gnn_done", "xin": "x_loaded",
            "took": "residual_taken", "resx": "residual_loaded", "tab": "table_stored",
            "adj0": "adjacency_loaded0", "adj1": "adjacency_loaded1", "adjf": "adjacency_used",
            "adjm": "mask_adjacency_loaded", "adjmf": "mask_adjacency_used",
            "idx": "slot_indices_ready", "gat0": "neighbours_fetched0", "gat1": "neighbours_fetched1",
            "gf": "neighbours_used", "aggr": "aggregate_ready", "q1": "first_part_ready",
            "parts": "parts_ready", "pd": "parts_stored", "stack": "stacks_loaded",
            "dl": "router_input_ready", "ed": "router_exp_ready", "wts": "expert_weights_ready",
            "mp": "max_parts_ready", "ms": "max_rows_stacked", "out": "stored"}.items()}

        begin = {n: 1 for n in free} | {"out": 16, "ring": {}}
        zeroth = Pass(begin, False, False, True)
        first = Pass(zeroth.after(1), False, True, True)
        middle = Pass(first.after(1), True, True, True)
        LOOPS = GRAPHS - 2
        sixth = Pass(middle.after(LOOPS), True, True, False)
        last = Pass(sixth.after(1), True, False, False)

        def over_passes(eng, body):
            body(zeroth, 0, -2)
            body(first, 0, -1)
            with eng.Fori(0, LOOPS) as b:
                body(middle, b, b)
            body(sixth, 0, GRAPHS - 2)
            body(last, 0, GRAPHS - 1)

        def key_of(ps, name, key):
            if isinstance(key, tuple) and key[0] in KEYED:
                return (name, key)
            return key

        def reached(ps, turn, name, key=None):
            here = ps.place[key_of(ps, name, key)][1] if key is not None else 0
            return turn * ps.count.get(name, 0) + (ps.start.get(name, 0) + here)

        def at(ps, turn, name, key=None):
            return S[name], reached(ps, turn, name, key)

        def psum(ps, key):
            n, i = ps.bank[key]
            return ring_banks[n][i]

        def ring_place(ps, turn, key):
            n, i = ps.bank[key]
            name = f"{n}{i}"
            k = (name, key) if isinstance(key, tuple) and key[0] in KEYED else key
            return name, turn * ps.count[name] + (ps.start.get(name, 1) + ps.place[k][1])

        def is_free(ps, turn, key):
            name, v = ring_place(ps, turn, key)
            return free[name], v - 1

        def is_taken(ps, turn, key):
            name, v = ring_place(ps, turn, key)
            return free[name], v

        def is_full(ps, turn, key):
            name, v = ring_place(ps, turn, key)
            return full[name], v - 1

        def filled(ps, key):
            n, i = ps.bank[key]
            return full[f"{n}{i}"], 1

        def emptied(ps, key):
            n, i = ps.bank[key]
            return free[f"{n}{i}"], 1

        x_v = x.rearrange("b (t p) c -> b p t c", p=P)
        adj_v = adj.rearrange("b (t p) m -> b t p m", p=P)
        out_v = out.rearrange("b (t p) c -> b p t c", p=P)
        parts_v = parts_dram.rearrange("s k (h d) n -> s k d h n", d=D)
        half = [slice(0, HALF), slice(HALF, NODES)]
        htiles = [slice(0, HTILES), slice(HTILES, TILES)]
        block = ctx.enter_context(nc.Block())

        def held_by(eng, pad, pool=False):
            if pool:
                eng.tensor_tensor(pad[0:1, 0:1], pad[0:1, 1:2], pad[0:1, 2:3], ALU.add)
                eng.drain()
            else:
                eng.memset(pad[0:1, 0:1], 0.0)

        loads = [
            (gW_sb[:, :, :], gW.rearrange("(k p) c -> p k c", p=P)), (Wg_sb[:, :], Wg),
            (W1_sb[:, :, :], W1.rearrange("e p h -> p e h")),
            (W2_sb[:, :, :, :], W2.rearrange("e (k p) c -> p e k c", p=P)),
            (Wat_sb[:, 0, :], Wq), (Wat_sb[:, 1, :], Wk), (Wat_sb[:, 2, :], Wv), (Wat_sb[:, 3, :], Wo),
            (rw1_sb[:, :], rw1), (rw2_sb[:, :], rw2),
            (ew_sb[:, 0, :, :], ew1.rearrange("e p h -> p e h")),
            (ew_sb[:, 1, :, :], ew2.rearrange("e p h -> p e h")),
            (ew_sb[:, 2, :, :], ew3.rearrange("e p h -> p e h")),
            (gb_b[:, :], gb.partition_broadcast(P)), (bo_b[:, :], bo.partition_broadcast(P)),
            (bg_b[:, :], bg.partition_broadcast(P)), (rb2_b[:, :], rb2.partition_broadcast(P)),
        ]
        late_loads = [
            (bias_rows[0:E0 * HC, :], b1.rearrange("e (k p) -> (e k) p", p=P)),
            (bias_rows[EB1:EB1 + E1, :], eb1), (bias_rows[EB2:EB2 + E1, :], eb2),
            (bias_rows[RB1:RB1 + 1, 0:RH], rb1.rearrange("(a n) -> a n", a=1)),
        ]
        for t in range(TILES):
            late_loads.append((bias_diag[t * EP:t * EP + E0, t % HTILES, :], b2))
            late_loads.append((bias_diag[(TILES + t) * EP:(TILES + t) * EP + E1, t % HTILES, :], eb3))
        N_LOADS = 16 * (len(loads) + len(late_loads))
        N_CONST = 6

        @block.sync
        def _(sp):
            sp.wait_ge(s_const, N_CONST)
            sp.dma_start(table[NODES:ROWS, :], zrows).then_inc(S["out"], 16)

            def body(ps, turn, b):
                for step in ps.steps:
                    kind = step[0]
                    if kind == "load_x":
                        if ps.front:
                            sp.wait_ge(*is_taken(ps, turn, ("xn", 1)))
                        sp.dma_start(xn0[:, :, :], x_v[b + 2, :, :, :]).then_inc(S["xin"], 16)
                        if ps is zeroth:
                            for dst, src in loads + late_loads:
                                sp.dma_start(dst, src).then_inc(s_w, 16)
                    elif kind == "load_res":
                        if ps.back:
                            sp.wait_ge(*at(ps, turn, "took", ("take",)))
                        sp.dma_start(res_n[:, :, :], x_v[b + 1, :, :, :]).then_inc(S["resx"], 16)
                    elif kind == "store_x":
                        sp.wait_ge(*at(ps, turn, "xn0", ("ln", 0)))
                        sp.dma_start(table[0:NODES, :].rearrange("(t p) c -> p t c", p=P),
                                     xn0[:, :, :]).then_inc(S["tab"], 16)
                    elif kind == "load_adj":
                        t = step[1]
                        if t >= 2:
                            sp.wait_ge(*at(ps, turn, "adjf", ("find", t - 2, 0)))
                        elif ps is not zeroth:
                            sp.wait_ge(*at(ps, turn, "adjf"))
                        sp.dma_start(adj_sb[:, t % 2, :], adj_v[b + 2, t, :, :]).then_inc(S[f"adj{t % 2}"], 16)
                    elif kind == "load_mask":
                        t = step[1]
                        if t >= 1:
                            sp.wait_ge(*at(ps, turn, "adjmf", ("mask", t - 1)))
                        elif ps is not middle:
                            sp.wait_ge(*at(ps, turn, "adjmf"))
                        else:
                            sp.wait_ge(*at(ps, turn, "x1"))
                        sp.dma_start(adjm[:, :], adj_v[b, t, :, :]).then_inc(S["adjm"], 16)
                    elif kind == "qk":
                        i = step[1]
                        sp.wait_ge(*at(ps, turn, "parts", step))
                        sp.dma_start(parts_dram[i, :, :, :].rearrange("k p n -> p k n"),
                                     parts[:, :, :]).then_inc(S["pd"], 16)
                        sp.wait_ge(*at(ps, turn, "pd", step))
                        stack, which = ((QS, QPART), (KS, KPART))[i]
                        for j, k in enumerate(which):
                            sp.dma_start(stack[D * j:D * j + D, :, :],
                                         parts_v[i, k, :, :, :]).then_inc(S["stack"], 16)
                    elif kind == "mT":
                        sp.wait_ge(*is_taken(ps, turn, "mT"))
                        for k in range(PARTS):
                            sp.dma_start(QS[SROWS + k:SROWS + k + 1, :, :].rearrange("o h n -> o (h n)"),
                                         mT[0:HEADS * TILES, k, :]).then_inc(S["ms"], 16)
                    elif kind == "store":
                        sp.wait_ge(*is_taken(ps, turn, ("y1", len(ORDER1) - 1)))
                        sp.dma_start(out_v[b, :, :, :], res_b[:, :, :]).then_inc(S["out"], 16)

            over_passes(sp, body)
            sp.wait_ge(S["out"], 16 * GRAPHS + 16)

        @block.gpsimd
        def _(pool):
            pool.memset(ident[:, :], 0.0).then_inc(s_ident, 1)
            pool.memset(identb[:, :], 0.0).then_inc(s_ident, 1)
            pool.memset(pool_pad[:, :], 0.0).then_inc(s_ident, 1)
            pool.memset(tmp[:, 0:2 * P], 0.0).then_inc(s_const, 1)
            pool.memset(bias_diag[:, :, :], 0.0).then_inc(s_const, 1)
            pool.iota(countdown[:, :], pattern=[[-1, NODES]], base=NODES, channel_multiplier=0,
                      allow_small_or_imprecise_dtypes=True).then_inc(s_const, 1)
            pool.iota(eidx[:, :, :], pattern=[[0, TILES], [1, EP]], base=0, channel_multiplier=0,
                      allow_small_or_imprecise_dtypes=True).then_inc(s_const, 1)
            pool.wait_ge(s_ident, 3)
            for m in (ident, identb):
                pool.affine_select(out=m[:, :], in_=m[:, :], compare_op=ALU.not_equal, fill=1.0,
                                   base=0, pattern=[[-1, P]], channel_multiplier=1).then_inc(s_const, 1)
            pool.wait_ge(s_const, N_CONST)
            pool.wait_ge(S["out"], 16)

            def body(ps, turn, b):
                if ps.near:
                    pool.wait_ge(*at(ps, turn, "tab", ("store_x",)))
                    for t in range(TILES):
                        pool.wait_ge(*at(ps, turn, "idx", ("find", t, 1)))
                        held_by(pool, pool_pad, True)
                        if t >= 2:
                            pool.wait_ge(*at(ps, turn, "gf", ("pmax", t - 2)))
                            held_by(pool, pool_pad, True)
                        for s in range(SLOTS):
                            pool.indirect_dma_start(
                                G[:, t % 2, s, :], None, table,
                                bass.IndirectOffsetOnAxis(slot_idx[:, t, s:s + 1], axis=0),
                                bounds_check=ROWS - 1, oob_is_err=False).then_inc(S[f"gat{t % 2}"], 16)

            over_passes(pool, body)

        @block.vector
        def _(dve):
            def settle(ins):
                dve.drain()
                return ins

            def norm(ps, turn, step, src, dst, signal=True):
                for t in range(TILES):
                    dve.bn_stats(st[:, t, :], src[:, t, :])
                dve.drain()
                for t in range(TILES):
                    dve.bn_aggr(mv[:, t, :], st[:, t, :])
                dve.drain()
                settle(dve.tensor_scalar(sd[:, :], mv[:, :, 1], EPS, None, ALU.add).then_inc(S["var"], 1))
                dve.wait_ge(*at(ps, turn, "sq", step))
                settle(dve.reciprocal(rstd[:, :], sq[:, :]))
                for t in range(TILES):
                    ins = dve.tensor_scalar(dst[:, t, :], src[:, t, :], mv[:, t, 0:1], rstd[:, t:t + 1],
                                            ALU.subtract, ALU.mult)
                if signal:
                    ins.then_inc(S["xn0" if step[1] == 0 else "xn"], 1)
                dve.drain()

            def ln(ps, turn, step):
                if step[1] == 0:
                    dve.wait_ge(*at(ps, turn, "xin", ("load_x",)))
                    norm(ps, turn, step, xn0, xn0)
                elif step[1] == 1:
                    if ps.back:
                        dve.wait_ge(*is_taken(ps, turn, ("tq", 1)))
                    norm(ps, turn, step, res_n, xn)
                elif step[1] == 2:
                    norm(ps, turn, step, res_b, xn, False)
                    for t in range(TILES):
                        ins = dve.tensor_scalar(XQ[:, t, :], xn[:, t, :], keeps[0][:, t:t + 1], None, ALU.mult)
                    settle(ins.then_inc(S["xn"], 1))
                else:
                    norm(ps, turn, step, res_b, xn)

            def find(ps, turn, t, part):
                tp = top[:, t % 2, :]
                if part == 0:
                    dve.wait_ge(*at(ps, turn, f"adj{t % 2}", ("load_adj", t)))
                    settle(dve.scalar_tensor_tensor(out=score[:, :], in0=adj_sb[:, t % 2, :], scalar=0,
                                                    in1=countdown[:, :], op0=ALU.not_equal,
                                                    op1=ALU.mult).then_inc(S["adjf"], 1))
                for r in (range(0, 2) if part == 0 else range(2, ROUNDS)):
                    settle(dve.max(tp[:, 8 * r:8 * r + 8], score[:, :]))
                    if r < ROUNDS - 1:
                        settle(dve.match_replace(score[:, :], tp[:, 8 * r:8 * r + 8], score[:, :], 0.0))
                if part == 1:
                    dve.tensor_scalar(slot_idx[:, t, :], tp[:, 0:SLOTS], -1.0, float(NODES),
                                      ALU.mult, ALU.add).then_inc(S["idx"], 1)
                    dve.tensor_scalar(keeps[2][:, t:t + 1], tp[:, 0:1], 0.0, None, ALU.is_gt)
                    settle(dve.tensor_scalar(floor[:, t:t + 1], tp[:, SLOTS:SLOTS + 1], 0.0, LOWEST,
                                             ALU.is_gt, ALU.mult))

            def pool_max(ps, turn, t):
                dve.wait_ge(*at(ps, turn, f"gat{t % 2}", ("pmax", t)))
                settle(dve.tensor_reduce(out=agg[:, t, :], in_=G[:, t % 2, :, :].rearrange("p s c -> p c s"),
                                         axis=AX.X, op=ALU.max).then_inc(S["gf"], 1))
                settle(dve.tensor_scalar(agg[:, t, :], agg[:, t, :], floor[:, t:t + 1], None,
                                         ALU.max).then_inc(S["aggr"], 1))

            def gnn_add(ps, turn):
                dve.wait_ge(*at(ps, turn, "resx", ("load_res",)))
                held_by(dve, dve_pad)
                for hf in range(2):
                    key = ("gnn", hf)
                    dve.wait_ge(*is_full(ps, turn, key))
                    y = psum(ps, key)[:, :].rearrange("p (t c) -> p t c", c=C)
                    tm = tmp[:, :].rearrange("p (t c) -> p t c", c=C)
                    ins = dve.tensor_tensor(tm, y, gb_b[:, :].unsqueeze(1).to_broadcast([P, HTILES, C]), ALU.add)
                    ins.then_inc(*emptied(ps, key))
                    dve.drain()
                    ins = dve.scalar_tensor_tensor(out=res_n[:, htiles[hf], :], in0=tm, scalar=0.0,
                                                   in1=res_n[:, htiles[hf], :], op0=ALU.max, op1=ALU.add)
                    if hf == 1:
                        ins.then_inc(S["x1"], 1)
                    dve.drain()

            def choose(ps, turn, step):
                layer = step[1]
                if layer == 0:
                    dve.wait_ge(*is_full(ps, turn, "lg0"))
                    ins = dve.tensor_tensor(lg[:, :, 0:E0],
                                            psum(ps, "lg0")[:, 0:TILES * E0].rearrange("p (t e) -> p t e", e=E0),
                                            bg_b[:, :].unsqueeze(1).to_broadcast([P, TILES, E0]), ALU.add)
                    ins.then_inc(*emptied(ps, "lg0"))
                    dve.drain()
                    values = lg
                else:
                    dve.wait_ge(*is_full(ps, turn, "lg1"))
                    ins = dve.tensor_tensor(lg[:, :, 0:E1],
                                            psum(ps, "lg1")[:, 0:TILES * E1].rearrange("p (t e) -> p t e", e=E1),
                                            rb2_b[:, :].unsqueeze(1).to_broadcast([P, TILES, E1]), ALU.add)
                    ins.then_inc(*emptied(ps, "lg1"))
                    dve.drain()
                    settle(dve.tensor_reduce(out=dlt[:, :], in_=lg[:, :, 0:E1], axis=AX.X, op=ALU.max))
                    settle(dve.tensor_tensor(lg[:, :, 0:E1], lg[:, :, 0:E1],
                                             dlt[:, :].unsqueeze(2).to_broadcast([P, TILES, E1]),
                                             ALU.subtract).then_inc(S["dl"], 1))
                    dve.wait_ge(*at(ps, turn, "ed", ("sm",)))
                    settle(dve.tensor_reduce(out=dlt[:, :], in_=ex[:, :, 0:E1], axis=AX.X, op=ALU.add))
                    settle(dve.reciprocal(dlt[:, :], dlt[:, :]))
                    settle(dve.tensor_tensor(pr_sb[:, :, 0:E1], ex[:, :, 0:E1],
                                             dlt[:, :].unsqueeze(2).to_broadcast([P, TILES, E1]), ALU.mult))
                    values = pr_sb
                for t in range(TILES):
                    dve.max(best[:, t, :], values[:, t, :])
                dve.drain()
                for t in range(TILES):
                    dve.max_index(besti[:, t, :], best[:, t, :], values[:, t, :])
                settle(dve.tensor_tensor(dlt[:, :], best[:, :, 1], best[:, :, 0],
                                         ALU.subtract).then_inc(S["dl"], 1))
                settle(dve.tensor_copy(bestf[:, :, 0:2], besti[:, :, 0:2]))
                for i in range(2):
                    dve.tensor_tensor(pick[:, i, :, :], eidx[:, :, :],
                                      bestf[:, :, i:i + 1].to_broadcast([P, TILES, EP]), ALU.is_equal)
                dve.drain()
                dve.wait_ge(*at(ps, turn, "ed", step))
                settle(dve.tensor_scalar(w1st[:, :], ed[:, :], 1.0, None, ALU.add))
                settle(dve.reciprocal(w1st[:, :], w1st[:, :]))
                settle(dve.tensor_tensor(w2nd[:, :], ed[:, :], w1st[:, :], ALU.mult))
                for i, w in enumerate((w1st, w2nd)):
                    dve.tensor_tensor(pick[:, i, :, :], pick[:, i, :, :],
                                      w[:, :].unsqueeze(2).to_broadcast([P, TILES, EP]), ALU.mult)
                dve.drain()
                settle(dve.tensor_tensor(wts[layer][:, layer * TILES:(layer + 1) * TILES, :], pick[:, 0, :, :], pick[:, 1, :, :],
                                         ALU.add).then_inc(S["wts"], 1))
                key = f"wT{layer}"
                dve.wait_ge(*is_full(ps, turn, key))
                mine = slice(layer * TILES * EP, (layer + 1) * TILES * EP)
                dve.tensor_copy(WT[mine, :], psum(ps, key)[mine, 0:P]).then_inc(*emptied(ps, key))
                dve.drain()
                res = (res_n, res_b)[layer]
                for hf in range(2):
                    key = ("b", layer, hf)
                    dve.wait_ge(*is_full(ps, turn, key))
                    ins = dve.tensor_tensor(res[:, htiles[hf], :], res[:, htiles[hf], :],
                                            psum(ps, key)[:, :].rearrange("p (t c) -> p t c", c=C), ALU.add)
                    ins.then_inc(*emptied(ps, key))
                dve.drain()

            def combine(ps, turn, layer, i):
                hf, e = (ORDER0, ORDER1)[layer][i]
                res = (res_n, res_b)[layer]
                key = (f"y{layer}", i)
                dve.wait_ge(*is_full(ps, turn, key))
                for tt in range(HTILES):
                    t = hf * HTILES + tt
                    ins = dve.scalar_tensor_tensor(out=res[:, t, :], in0=psum(ps, key)[:, tt * C:(tt + 1) * C],
                                                   scalar=wts[layer][:, layer * TILES + t, e:e + 1], in1=res[:, t, :],
                                                   op0=ALU.mult, op1=ALU.add)
                ins.then_inc(*emptied(ps, key))
                dve.drain()

            def split_parts(ps, turn, i):
                for hf in range(2):
                    cols = half[hf]
                    key = ("qk", i, hf)
                    dve.wait_ge(*at(ps, turn, "q1", ("q1", i, hf)))
                    ins = dve.tensor_tensor(rest[:, :], psum(ps, key)[:, :], parts[:, 0, cols], ALU.subtract)
                    ins.then_inc(*emptied(ps, key))
                    dve.drain()
                    settle(dve.tensor_copy(parts[:, 1, cols], rest[:, :]))
                    ins = dve.tensor_tensor(parts[:, 2, cols], rest[:, :], parts[:, 1, cols], ALU.subtract)
                    if hf == 1:
                        ins.then_inc(S["parts"], 1)
                    dve.drain()

            dve.wait_ge(s_const, N_CONST)
            for bank in free.values():
                dve.memset(dve_pad[:, 0:1], 0.0).then_inc(bank, 1)
                dve.drain()
            dve.memset(VS[:, :, :], 0.0)
            dve.memset(KS[SROWS:SROWS + PARTS, :, :], 1.0)
            dve.memset(mparts[:, :, :], 0.0)
            dve.memset(lg[:, :, :], -1.0)
            dve.memset(pr_sb[:, :, :], -1.0)
            for w in wts:
                dve.memset(w[:, :, :], 0.0)
            for k in keeps:
                dve.memset(k[:, :], 0.0)
            dve.drain()
            dve.memset(VH[:, :, :, D:D + 1], 1.0)
            dve.drain()

            def body(ps, turn, b):
                if ps is first:
                    dve.wait_ge(s_btp, 1)
                    settle(dve.tensor_copy(bias_T[:, :], ring_banks["M"][0][:, 0:P]).then_inc(s_bt, 1))
                for i in range(2):
                    settle(dve.tensor_copy(keeps[i][:, :], keeps[i + 1][:, :]))
                settle(dve.tensor_scalar(drop[:, :], keeps[0][:, :], -BIG, None, ALU.mult))
                for step in ps.steps:
                    kind = step[0]
                    if kind == "ln":
                        ln(ps, turn, step)
                    elif kind == "find":
                        find(ps, turn, step[1], step[2])
                    elif kind == "pmax":
                        pool_max(ps, turn, step[1])
                    elif kind == "gnn_add":
                        gnn_add(ps, turn)
                    elif kind == "choose":
                        choose(ps, turn, step)
                    elif kind == "acc0":
                        combine(ps, turn, 0, step[1])
                    elif kind == "acc1":
                        combine(ps, turn, 1, step[1])
                    elif kind == "take":
                        dve.wait_ge(*at(ps, turn, "out"))
                        settle(dve.tensor_copy(res_b[:, :, :], res_n[:, :, :]).then_inc(S["took"], 1))
                    elif kind == "qk":
                        split_parts(ps, turn, step[1])
                    elif kind == "mask":
                        t = step[1]
                        dve.wait_ge(*at(ps, turn, "adjm", ("load_mask", t)))
                        settle(dve.tensor_scalar(mask[:, t, :], adjm[:, :], 0, drop[:, t:t + 1],
                                                 ALU.is_le, ALU.mult).then_inc(S["adjmf"], 1))
                    elif kind == "s":
                        _, t, h = step
                        dve.wait_ge(*is_full(ps, turn, step))
                        if (t, h) == (0, 0):
                            held_by(dve, dve_pad[:, 1:2])
                            dve.wait_ge(*at(ps, turn, "stack", ("qk", 1)))
                        held_by(dve, dve_pad)
                        ins = dve.tensor_tensor_reduce(out=junk, in0=psum(ps, step)[:, :], in1=mask[:, t, :],
                                                       scale=1.0, scalar=LOWEST, op0=ALU.add, op1=ALU.max,
                                                       accum_out=MX[:, h, t:t + 1])
                        ins.then_inc(*emptied(ps, step))
                        dve.drain()
                    elif kind == "mparts":
                        mx = MX[:, :, :].rearrange("p h t -> p (h t)")
                        settle(dve.tensor_scalar(mrest[:, :], mx, -1.0, None, ALU.mult))
                        for k in range(PARTS):
                            ins = dve.tensor_copy(mparts[:, k, 0:HEADS * TILES], mrest[:, :])
                            if k == PARTS - 1:
                                ins.then_inc(S["mp"], 1)
                            dve.drain()
                            if k < PARTS - 1:
                                settle(dve.tensor_tensor(mrest[:, :], mrest[:, :],
                                                         mparts[:, k, 0:HEADS * TILES], ALU.subtract))
                    elif kind == "mT":
                        dve.wait_ge(*is_full(ps, turn, "mT"))
                        ins = dve.tensor_copy(mT[:, :, :].rearrange("p k n -> p (k n)"),
                                              psum(ps, "mT")[:, :].bitcast(BF16)[:, 0:PARTS * P])
                        ins.then_inc(*emptied(ps, "mT"))
                        dve.drain()
                    elif kind == "fin":
                        _, qh, g = step
                        key = ("av", qh, g)
                        dve.wait_ge(*is_full(ps, turn, key))
                        dve.tensor_copy(CT[:, :], psum(ps, key)[:, :]).then_inc(*emptied(ps, key))
                        dve.drain()
                        key = ("ctx", qh, g)
                        dve.wait_ge(*is_full(ps, turn, key))
                        c4 = psum(ps, key)[:, :].rearrange("p (q h d) -> p q h d", h=GH, d=32)
                        settle(dve.reciprocal(rden[:, :, :], c4[:, :, :, D]))
                        cn = ctxn[:, :, g * GH * D:(g + 1) * GH * D].rearrange("p q (h d) -> p q h d", d=D)
                        ins = dve.tensor_tensor(cn, c4[:, :, :, 0:D],
                                                rden[:, :, :].unsqueeze(3).to_broadcast([P, HTILES, GH, D]), ALU.mult)
                        ins.then_inc(*emptied(ps, key))
                        dve.drain()
                    elif kind == "proj":
                        qh = step[1]
                        key = ("proj", qh)
                        dve.wait_ge(*is_full(ps, turn, key))
                        y = psum(ps, key)[:, :].rearrange("p (t c) -> p t c", c=C)
                        ins = dve.tensor_tensor(res_b[:, htiles[qh], :], res_b[:, htiles[qh], :], y, ALU.add)
                        ins.then_inc(*emptied(ps, key))
                        dve.drain()
                        settle(dve.tensor_tensor(res_b[:, htiles[qh], :], res_b[:, htiles[qh], :],
                                                 bo_b[:, :].unsqueeze(1).to_broadcast([P, HTILES, C]), ALU.add))

            over_passes(dve, body)

        @block.scalar
        def _(act):
            def copy_out(dst, ps, turn, key):
                act.wait_ge(*is_full(ps, turn, key))
                act.activation(dst, psum(ps, key)[:, :], ACT.Copy).then_inc(*emptied(ps, key))

            def body(ps, turn, b):
                for step in ps.steps:
                    kind = step[0]
                    if kind == "ln":
                        act.wait_ge(*at(ps, turn, "var", step))
                        act.activation(sq[:, :], sd[:, :], ACT.Sqrt).then_inc(S["sq"], 1)
                    elif kind == "gnn":
                        for hf in range(2):
                            copy_out(XT[:, half[hf]], ps, turn, ("xn", hf))
                            copy_out(XT2[:, half[hf]], ps, turn, ("agg", hf))
                    elif kind == "qT":
                        for hf in range(2):
                            copy_out(XB[:, half[hf]], ps, turn, ("ta", hf))
                        for hf in range(2):
                            copy_out(XT2[:, half[hf]], ps, turn, ("tq", hf))
                    elif kind == "qk":
                        i = step[1]
                        for hf in range(2):
                            key = ("qk", i, hf)
                            act.wait_ge(*is_full(ps, turn, key))
                            if i == 1 and hf == 0:
                                act.wait_ge(*at(ps, turn, "pd", ("qk", 0)))
                            act.activation(parts[:, 0, half[hf]], psum(ps, key)[:, :],
                                           ACT.Copy).then_inc(S["q1"], 1)
                    elif kind == "v":
                        for hf in range(2):
                            key = ("v", hf)
                            act.wait_ge(*is_full(ps, turn, key))
                            act.activation(VH[:, htiles[hf], :, 0:D],
                                                   psum(ps, key)[:, :].rearrange("p (t h d) -> p t h d", h=HEADS, d=D),
                                                   ACT.Copy).then_inc(*emptied(ps, key))
                    elif kind == "t0":
                        for hf in range(2):
                            copy_out(XT[:, half[hf]], ps, turn, ("t0", hf))
                    elif kind == "choose":
                        if step[1] == 1:
                            act.wait_ge(*at(ps, turn, "dl", ("sm",)))
                            act.activation(ex[:, :, 0:E1], lg[:, :, 0:E1], ACT.Exp).then_inc(S["ed"], 1)
                        act.wait_ge(*at(ps, turn, "dl", step))
                        act.activation(ed[:, :], dlt[:, :], ACT.Exp).then_inc(S["ed"], 1)
                    elif kind == "up0":
                        _, i, c = step
                        hf, e = ORDER0[i]
                        act.wait_ge(*is_full(ps, turn, step))
                        act.activation(HB[:, i % 2, c, :], psum(ps, step)[:, :], ACT.Gelu,
                                               bias=bias_T[:, e * HC + c:e * HC + c + 1]).then_inc(*emptied(ps, step))
                    elif kind == "st":
                        _, qh, g, kc = step
                        for pr in range(2):
                            key = (*step, pr)
                            act.wait_ge(*is_full(ps, turn, key))
                            act.activation(HB[:, kc % 2, 2 * pr:2 * pr + 2, :],
                                                   psum(ps, key)[:, :].rearrange("p (h q) -> p h q", h=2),
                                                   ACT.Exp, scale=float(D) ** -0.5).then_inc(*emptied(ps, key))
                    elif kind == "proj":
                        copy_out(XB[:, half[step[1]]], ps, turn, ("ctxT", step[1]))
                    elif kind == "t1":
                        for hf in range(2):
                            copy_out(XB[:, half[hf]], ps, turn, ("t1", hf))
                        for hf in range(2):
                            key = ("r1", hf)
                            act.wait_ge(*is_full(ps, turn, key))
                            act.activation(XT2[0:RH, half[hf]], psum(ps, key)[0:RH, :], ACT.Relu,
                                                   bias=bias_T[0:RH, RB1:RB1 + 1]).then_inc(*emptied(ps, key))
                    elif kind in ("u1", "u2"):
                        j = step[1]
                        hf, e = ORDER1[j]
                        act.wait_ge(*is_full(ps, turn, step))
                        k, col = (0, EB1) if kind == "u1" else (2, EB2)
                        act.activation(HB[:, 0, k + j % 2, :], psum(ps, step)[:, :], ACT.Relu,
                                               bias=bias_T[:, col + e:col + e + 1]).then_inc(*emptied(ps, step))

            over_passes(act, body)

        @block.tensor
        def _(pe):
            def transposes(ps, turn, key, src, hf):
                pe.wait_ge(*is_free(ps, turn, key))
                for tt in range(HTILES):
                    ins = pe.transpose(psum(ps, key)[:, tt * P:(tt + 1) * P], src[:, hf * HTILES + tt, :], ident[:, :])
                ins.then_inc(*filled(ps, key))

            def rows_times(ps, turn, key, srcT, hf, weight):
                pe.wait_ge(*is_free(ps, turn, key))
                for tt in range(HTILES):
                    t = hf * HTILES + tt
                    ins = pe.matmul(psum(ps, key)[:, tt * C:(tt + 1) * C], srcT[:, t * P:(t + 1) * P], weight,
                                    start=True, stop=True)
                ins.then_inc(*filled(ps, key))

            def body(ps, turn, b):
                if ps is first:
                    pe.wait_ge(s_w, N_LOADS)
                    pe.wait_ge(s_const, N_CONST)
                    pe.transpose(ring_banks["M"][0][:, 0:P], bias_rows, ident[:, :]).then_inc(s_btp, 1)
                    pe.wait_ge(s_bt, 1)
                for step in ps.steps:
                    kind = step[0]
                    if kind == "gnn":
                        pe.wait_ge(*at(ps, turn, "xn0"))
                        pe.wait_ge(*at(ps, turn, "aggr"))
                        for hf in range(2):
                            transposes(ps, turn, ("xn", hf), xn0, hf)
                            transposes(ps, turn, ("agg", hf), agg, hf)
                            pe.wait_ge(*is_taken(ps, turn, ("xn", hf)))
                            pe.wait_ge(*is_taken(ps, turn, ("agg", hf)))
                            key = ("gnn", hf)
                            pe.wait_ge(*is_free(ps, turn, key))
                            for tt in range(HTILES):
                                t = hf * HTILES + tt
                                o = psum(ps, key)[:, tt * C:(tt + 1) * C]
                                pe.matmul(o, XT[:, t * P:(t + 1) * P], gW_sb[:, 0, :], start=True, stop=False)
                                ins = pe.matmul(o, XT2[:, t * P:(t + 1) * P], gW_sb[:, 1, :], start=False, stop=True)
                            ins.then_inc(*filled(ps, key))
                    elif kind == "qT":
                        pe.wait_ge(*at(ps, turn, "xn", ("ln", 2)))
                        for hf in range(2):
                            transposes(ps, turn, ("ta", hf), xn, hf)
                        for hf in range(2):
                            transposes(ps, turn, ("tq", hf), XQ, hf)
                    elif kind == "qk":
                        i = step[1]
                        src = (XT2, XB)[i]
                        for hf in range(2):
                            if i == 0:
                                pe.wait_ge(*is_taken(ps, turn, ("tq", hf)))
                            key = ("qk", i, hf)
                            pe.wait_ge(*is_free(ps, turn, key))
                            pe.matmul(psum(ps, key)[:, :], Wat_sb[:, i, :], src[:, half[hf]],
                                             start=True, stop=True).then_inc(*filled(ps, key))
                    elif kind == "v":
                        for hf in range(2):
                            rows_times(ps, turn, ("v", hf), XB, hf, Wat_sb[:, 2, :])
                    elif kind == "t0":
                        pe.wait_ge(*at(ps, turn, "xn", ("ln", 1)))
                        for hf in range(2):
                            transposes(ps, turn, ("t0", hf), xn, hf)
                        pe.wait_ge(*is_taken(ps, turn, ("t0", 0)))
                        pe.wait_ge(*is_taken(ps, turn, ("t0", 1)))
                        pe.wait_ge(*is_free(ps, turn, "lg0"))
                        for t in range(TILES):
                            ins = pe.matmul(psum(ps, "lg0")[:, t * E0:(t + 1) * E0], XT[:, t * P:(t + 1) * P],
                                            Wg_sb[:, :], start=True, stop=True)
                        ins.then_inc(*filled(ps, "lg0"))
                    elif kind == "choose":
                        layer = step[1]
                        pe.wait_ge(*at(ps, turn, "wts", step))
                        key = f"wT{layer}"
                        pe.wait_ge(*is_free(ps, turn, key))
                        pe.transpose(psum(ps, key)[:, 0:P], wts[layer][:, :, :].rearrange("p t e -> p (t e)"),
                                            ident[:, :]).then_inc(*filled(ps, key))
                        pe.wait_ge(*is_taken(ps, turn, key))
                        for hf in range(2):
                            key = ("b", layer, hf)
                            pe.wait_ge(*is_free(ps, turn, key))
                            first_row = (2 * layer + hf) * HTILES * EP
                            rows = slice(first_row, first_row + HTILES * EP)
                            pe.matmul(psum(ps, key)[:, :], WT[rows, :],
                                             bias_diag[rows, :, :].rearrange("k t c -> k (t c)"),
                                             start=True, stop=True).then_inc(*filled(ps, key))
                    elif kind == "up0":
                        _, i, c = step
                        hf, e = ORDER0[i]
                        pe.wait_ge(*is_free(ps, turn, step))
                        pe.matmul(psum(ps, step)[:, :], W1_sb[:, e, c * P:(c + 1) * P], XT[:, half[hf]],
                                         start=True, stop=True).then_inc(*filled(ps, step))
                    elif kind == "down0":
                        _, i, tt = step
                        hf, e = ORDER0[i]
                        key = ("y0", i)
                        if tt == 0:
                            for c in (HC - 2, HC - 1):
                                pe.wait_ge(*is_taken(ps, turn, ("up0", i, c)))
                            pe.wait_ge(*is_free(ps, turn, key))
                        for c in range(HC):
                            ins = pe.matmul(psum(ps, key)[:, tt * C:(tt + 1) * C],
                                            HB[:, i % 2, c, tt * P:(tt + 1) * P], W2_sb[:, e, c, :],
                                            start=(c == 0), stop=(c == HC - 1))
                        if tt == HTILES - 1:
                            ins.then_inc(*filled(ps, key))
                    elif kind == "s":
                        _, t, h = step
                        if (t, h) == (0, 0):
                            pe.wait_ge(*at(ps, turn, "stack", ("qk", 1)))
                        pe.wait_ge(*is_free(ps, turn, step))
                        for hf in range(2):
                            ins = pe.matmul(psum(ps, step)[:, half[hf]], QS[0:SROWS, h, t * P:(t + 1) * P],
                                            KS[0:SROWS, h, half[hf]], start=True, stop=True)
                        ins.then_inc(*filled(ps, step))
                    elif kind == "mT":
                        pe.wait_ge(*at(ps, turn, "mp", ("mparts",)))
                        pe.wait_ge(*is_free(ps, turn, "mT"))
                        for k in range(PARTS):
                            ins = pe.transpose(psum(ps, "mT")[:, :].bitcast(BF16)[:, k * P:(k + 1) * P],
                                               mparts[:, k, :], identb[:, :])
                        ins.then_inc(*filled(ps, "mT"))
                    elif kind == "st":
                        _, qh, g, kc = step
                        if (qh, g, kc) == (0, 0, 0):
                            pe.wait_ge(*at(ps, turn, "ms", ("mT",)))
                        for pr in range(2):
                            key = (*step, pr)
                            pe.wait_ge(*is_free(ps, turn, key))
                            for hh in range(2):
                                h = g * GH + 2 * pr + hh
                                o = psum(ps, key)[:, half[hh]]
                                pe.matmul(o, KS[0:SROWS + PARTS, h, kc * P:(kc + 1) * P],
                                          QS[0:SROWS + PARTS, h, half[qh]], start=True, stop=False)
                                for qt in range(HTILES):
                                    ins = pe.matmul(o[:, qt * P:(qt + 1) * P],
                                                    mask[:, qh * HTILES + qt, kc * P:(kc + 1) * P], identb[:, :],
                                                    start=False, stop=(qt == HTILES - 1))
                            ins.then_inc(*filled(ps, key))
                    elif kind == "av":
                        _, qh, g, kc = step
                        for pr in range(2):
                            pe.wait_ge(*is_taken(ps, turn, ("st", qh, g, kc, pr)))
                        key = ("av", qh, g)
                        if kc == 0:
                            pe.wait_ge(*is_free(ps, turn, key))
                            if (qh, g) == (0, 0):
                                pe.wait_ge(*is_taken(ps, turn, ("v", 0)))
                                pe.wait_ge(*is_taken(ps, turn, ("v", 1)))
                        for hh in range(GH):
                            ins = pe.matmul(psum(ps, key)[32 * hh:32 * hh + 32, :], VS[:, kc, (D + 1) * (g * GH + hh):(D + 1) * (g * GH + hh) + 32],
                                            HB[:, kc % 2, hh, :], start=(kc == 0), stop=(kc == TILES - 1))
                        if kc == TILES - 1:
                            ins.then_inc(*filled(ps, key))
                    elif kind == "fin":
                        _, qh, g = step
                        pe.wait_ge(*is_taken(ps, turn, ("av", qh, g)))
                        key = ("ctx", qh, g)
                        pe.wait_ge(*is_free(ps, turn, key))
                        for tt in range(HTILES):
                            ins = pe.transpose(psum(ps, key)[:, tt * P:(tt + 1) * P], CT[:, tt * P:(tt + 1) * P],
                                               ident[:, :])
                        ins.then_inc(*filled(ps, key))
                    elif kind == "proj":
                        qh = step[1]
                        pe.wait_ge(*is_taken(ps, turn, ("ctx", qh, 0)))
                        pe.wait_ge(*is_taken(ps, turn, ("ctx", qh, 1)))
                        transposes(ps, turn, ("ctxT", qh), ctxn, 0)
                        pe.wait_ge(*is_taken(ps, turn, ("ctxT", qh)))
                        rows_times(ps, turn, ("proj", qh), XB, qh, Wat_sb[:, 3, :])
                    elif kind == "t1":
                        pe.wait_ge(*at(ps, turn, "xn", ("ln", 3)))
                        for hf in range(2):
                            transposes(ps, turn, ("t1", hf), xn, hf)
                        for hf in range(2):
                            pe.wait_ge(*is_taken(ps, turn, ("t1", hf)))
                            key = ("r1", hf)
                            pe.wait_ge(*is_free(ps, turn, key))
                            pe.matmul(psum(ps, key)[0:RH, :], rw1_sb[:, :], XB[:, half[hf]],
                                             start=True, stop=True).then_inc(*filled(ps, key))
                        pe.wait_ge(*is_taken(ps, turn, ("r1", 0)))
                        pe.wait_ge(*is_taken(ps, turn, ("r1", 1)))
                        pe.wait_ge(*is_free(ps, turn, "lg1"))
                        for t in range(TILES):
                            ins = pe.matmul(psum(ps, "lg1")[:, t * E1:(t + 1) * E1], XT2[0:RH, t * P:(t + 1) * P],
                                            rw2_sb[:, :], start=True, stop=True)
                        ins.then_inc(*filled(ps, "lg1"))
                    elif kind == "u1":
                        hf, e = ORDER1[step[1]]
                        pe.wait_ge(*is_free(ps, turn, step))
                        pe.matmul(psum(ps, step)[:, :], ew_sb[:, 0, e, :], XB[:, half[hf]],
                                         start=True, stop=True).then_inc(*filled(ps, step))
                    elif kind == "u2":
                        j = step[1]
                        hf, e = ORDER1[j]
                        pe.wait_ge(*is_taken(ps, turn, ("u1", j)))
                        pe.wait_ge(*is_free(ps, turn, step))
                        pe.matmul(psum(ps, step)[:, :], ew_sb[:, 1, e, :], HB[:, 0, j % 2, :],
                                         start=True, stop=True).then_inc(*filled(ps, step))
                    elif kind == "y1":
                        j = step[1]
                        hf, e = ORDER1[j]
                        pe.wait_ge(*is_taken(ps, turn, ("u2", j)))
                        pe.wait_ge(*is_free(ps, turn, step))
                        for tt in range(HTILES):
                            ins = pe.matmul(psum(ps, step)[:, tt * C:(tt + 1) * C],
                                            HB[:, 0, 2 + j % 2, tt * P:(tt + 1) * P], ew_sb[:, 2, e, :],
                                            start=True, stop=True)
                        ins.then_inc(*filled(ps, step))

            over_passes(pe, body)


_INS = ['x', 'adj', 'L0_gnn_W', 'L0_gnn_b', 'L0_ffn_Wg', 'L0_ffn_bg', 'L0_ffn_W1', 'L0_ffn_b1', 'L0_ffn_W2',
        'L0_ffn_b2', 'L1_gnn_Wq', 'L1_gnn_Wk', 'L1_gnn_Wv', 'L1_gnn_Wo', 'L1_gnn_bo', 'L1_ffn_router_w1',
        'L1_ffn_router_b1', 'L1_ffn_router_w2', 'L1_ffn_router_b2', 'L1_ffn_expert_w1', 'L1_ffn_expert_b1',
        'L1_ffn_expert_w2', 'L1_ffn_expert_b2', 'L1_ffn_expert_w3', 'L1_ffn_expert_b3']


def kernel(**inputs):
    import numpy as np
    import concourse.bacc as bacc
    from concourse.bass_utils import run_bass_kernel_spmd

    nc = bacc.Bacc("TRN2", target_bir_lowering=False, num_devices=1)
    arrays, args = {}, []
    for name in _INS:
        a = np.ascontiguousarray(inputs[name])
        arrays[f"in_{name}"] = a
        args.append(nc.dram_tensor(f"in_{name}", a.shape, mybir.dt.from_np(a.dtype), kind="ExternalInput").ap())
    out = nc.dram_tensor("out_x", (GRAPHS, NODES, C), F32, kind="ExternalOutput").ap()
    graph_kernel(nc, *args, out)
    r = run_bass_kernel_spmd(nc, [arrays], core_ids=[0])
    return r.results[0]["out_x"]
```

```python
from contextlib import ExitStack

import concourse.bass as bass
from concourse import mybir

F32 = mybir.dt.float32
BF16 = mybir.dt.bfloat16
F16 = mybir.dt.float16
U8 = mybir.dt.uint8
I32 = mybir.dt.int32
U32 = mybir.dt.uint32
ALU = mybir.AluOpType
ACT = mybir.ActivationFunctionType
AX = mybir.AxisListType

GRAPHS, NODES, C = 8, 1024, 128
P = 128
TILES = NODES // P
HALF = 512
HTILES = HALF // P
SLOTS = 25
TOP = 32
ROUNDS = TOP // 8
ROWS = NODES + 1
E0, HID0 = 8, 512
HC = HID0 // P
E1, RH = 6, 64
EP = 8
HEADS, D = 8, 16
PARTS = 3
PAIRS = 6
QPART = [0, 1, 0, 1, 2, 0]
KPART = [0, 0, 1, 1, 0, 2]
SROWS = PAIRS * D
GH = 4
BIG = float(2 ** 30)
LOWEST = -3.0e38
EPS = 1e-5


ORDER0 = [(hf, e) for hf in range(2) for e in range(E0)]
FINDS_EARLY = 10
ORDER1 = [(hf, e) for hf in range(2) for e in range(E1)]


CLASS_SLOTS = (8, 16)
UNITS_MIDDLE = 2
UNITS_LATE = 1


def spread(main, extra):
    s, done = [], 0
    for n, step in enumerate(main):
        s.append(step)
        upto = (n + 1) * len(extra) // len(main)
        s += extra[done:upto]
        done = upto
    return s + extra[done:]


def weave(scores, main, extra):
    s, tensor, vector, emptied = [], 0.0, 0.0, []
    scores, main, extra = list(scores), list(main), list(extra)
    every = (len([k for k in scores if k[0] == "s"]) * 1.35 + 15) / (len(extra) + 1)
    placed = 0
    while scores or main:
        if extra and tensor >= placed * every:
            placed += 1
            s.append(extra.pop(0))
            vector = max(vector, tensor) + {"find": 5.0 if s[-1][1:] != (0,) else 11.0, "pmax": 4.5}.get(s[-1][0], 0.0)
        elif scores and scores[0][0] != "s":
            if scores[0][0] == "mask":
                vector += 0.9
            s.append(scores.pop(0))
        elif scores and (len(emptied) < 2 or emptied[-2] <= tensor or not main):
            tensor = max(tensor, emptied[-2] if len(emptied) > 1 else 0.0) + 0.43
            vector = max(vector, tensor) + 1.3
            emptied.append(vector)
            s.append(scores.pop(0))
        else:
            if main[0][0] == "acc0":
                vector = max(vector, tensor) + 1.15
            else:
                tensor += 0.87
            s.append(main.pop(0))
    return s + extra


def schedule(att, unit, near, load):
    scores = []
    if att:
        for t in range(TILES):
            scores.append(("mask", t))
            if t + 1 < TILES:
                scores.append(("load_mask", t + 1))
            scores += [("s", t, h) for h in range(HEADS)]
    finds = []
    if near:
        finds += [("deg", 0), ("class", 0)]
        for t in range(TILES):
            finds.append(("find", t))
            if t + 2 < TILES:
                finds.append(("load_adj", t + 2))
            if t + 1 < TILES:
                finds.append(("deg", t + 1))
            if t >= 2:
                finds.append(("pmax", t - 2))
            if t + 1 < TILES:
                finds.append(("class", t + 1))
        finds.append(("pmax", TILES - 2))

    def experts0(mine):
        s = []
        for k in range(len(mine) + 1):
            if k < len(mine):
                s += [("up0", mine[k], c) for c in range(HC)]
            if k > 0:
                s += [("down0", mine[k - 1], tt) for tt in range(HTILES)] + [("acc0", mine[k - 1])]
        return s

    units = list(range(len(ORDER0))) if unit else []
    late = units[len(units) - UNITS_LATE:] if att and unit else []
    middle = units[len(units) - UNITS_LATE - UNITS_MIDDLE:-UNITS_LATE] if att and unit else []
    early = units[:len(units) - len(late) - len(middle)]
    groups = [(qh, g) for qh in range(2) for g in range(2)]
    second = []
    if att:
        second = [("mparts",), ("mT",)]
        for n, (qh, g) in enumerate(groups):
            for kc in range(TILES):
                second.append(("st", qh, g, kc))
                if kc == 1 and n > 0:
                    second.append(("fin", *groups[n - 1]))
                if kc == 3 and n == 2:
                    second.append(("proj", 0))
                if kc > 0:
                    second.append(("av", qh, g, kc - 1))
            second.append(("av", qh, g, TILES - 1))
    s = []
    main = experts0(early)
    if not att and not unit:
        s += finds
    elif not att:
        s += spread(main, finds)
    else:
        cut = FINDS_EARLY if finds else 0
        s += weave(scores, main, finds[:cut]) + second[:1] + experts0(middle[:1])
        s += second[1:2] + experts0(middle[1:])
        s += spread(second[2:], finds[cut:])

    late_up = [[("up0", k, c) for c in range(HC)] for k in late] + [[]] * 5
    late_down = [[("down0", k, tt) for tt in range(HTILES)] for k in late] + [[]] * 5
    late_acc = [[("acc0", k)] for k in late] + [[]] * 5
    if att:
        s += [("fin", 1, 1)] + late_up[0] + [("proj", 1), ("x2",), ("lnv", 3)]
    if near:
        s += [("pmax", TILES - 1)]
    s += late_down[0] + late_up[1]
    if att:
        s += [("ln", 3)]
    s += late_acc[0]
    if att:
        s += [("t1",)]
    s += late_down[1][:2]
    if att:
        s += [("r1",)]
    s += late_down[1][2:3]
    if near and not unit:
        s += [("bias",)]
    if near:
        s += [("gT",)]
    if att:
        s += [("lg1",)]
    s += late_down[1][3:]
    for n in range(2, len(late)):
        s += late_up[n] + late_acc[n - 1]
        if n == 2:
            s += [("cha", 1)]
        s += late_down[n]
    if near:
        s += [("gnn",)]
    if att and len(late) <= 2:
        s += [("cha", 1)]
    s += late_acc[max(1, len(late) - 1)]
    if unit:
        s += [("take",)]
    if near:
        s += [("load_res",)]
    chain = []
    if att and near:
        chain += [("chb", 1)]
    elif att:
        s += [("chb", 1)]
    if unit:
        chain += [("lnv", 2)]
    if near:
        chain += [("gnn_add",)]
    if att:
        chain += [("chc", 1)]
    if unit:
        chain += [("ln", 2)]
    chain += [("shift",)]
    if unit:
        chain += [("qT",)]
    if near:
        chain += [("lnv", 1)]
    if unit:
        chain += [("qk", 0)]
    if near:
        chain += [("ln", 1)]
    if unit:
        chain += [("qk", 1)]
    if near:
        chain += [("t0",)]
    if unit:
        chain += [("v",), ("next_mask",)]
    if near:
        chain += [("lg0",)]
    if load:
        chain += [("load_x",)]
    if near:
        chain += [("cha", 0), ("chb", 0), ("chc", 0)]
    if load:
        chain += [("lnv", 0), ("ln", 0), ("store_x",), ("next_adj", 0), ("next_adj", 1)]
    experts1 = []
    if att:
        n1 = len(ORDER1)
        for k in range(n1 + 3):
            if k < n1:
                experts1.append(("u1", k))
            if 1 <= k <= n1:
                experts1.append(("u2", k - 1))
            if 2 <= k <= n1 + 1:
                experts1.append(("y1", k - 2))
            if k >= 3:
                experts1.append(("acc1", k - 3))
    s += spread(experts1, chain) if experts1 else chain
    if att:
        assert s.index(("chb", 1)) < s.index(("acc1", 0))
        s.append(("store",))
    if load and not near:
        s.append(("load_w",))
    return s


def signals(step):
    k = step[0]
    H = lambda *key: [("H", key, 1)]
    Y = lambda *key: [("Y", key, 1)]
    A = lambda *key: [("A", key, 1)]
    if k == "lnv":
        return [("var", ("ln", step[1]), 1), ("sq", ("ln", step[1]), 1)]
    if k == "ln":
        return [("xn0" if step[1] == 0 else "xn", step, 1)]
    if k == "gT":
        return sum([H("xn", hf) + A("agg", hf) for hf in range(2)], [])
    if k == "gnn":
        return Y("gnn", 0) + Y("gnn", 1)
    if k == "gnn_add":
        return [("x1", step, 1)]
    if k == "take":
        return [("took", step, 1)]
    if k == "load_res":
        return [("resx", step, 16)]
    if k == "load_x":
        return [("xin", step, 16)]
    if k == "store_x":
        return [("tab", step, 16)]
    if k in ("load_adj", "next_adj"):
        return [(f"adj{step[1] % 2}", step, 16)]
    if k in ("load_mask", "next_mask"):
        return [("adjm", step, 16)]
    if k == "mask":
        return [("adjmf", step, 1)]
    if k == "find":
        return [("adjf", step, 1), ("idx", step, 1)]
    if k == "deg":
        return [("dg", step, 1)]
    if k == "class":
        return H(*step) + [("cat", step, 1)]
    if k == "pmax":
        return [(f"gat{step[1] % 2}", step, 16 * SLOTS), ("aggr", step, 1)]
    if k == "qT":
        return H("ta", 0) + H("ta", 1) + A("tq", 0) + A("tq", 1)
    if k == "qk":
        i = step[1]
        return (H("qk", i, 0) + H("qk", i, 1) + [("q1", ("q1", i, 0), 1), ("q1", ("q1", i, 1), 1),
                ("parts", step, 1), ("pd", step, 16), ("stack", step, 16 * PAIRS)])
    if k == "v":
        return H("v", 0) + H("v", 1)
    if k == "t0":
        return H("t0", 0) + H("t0", 1)
    if k == "t1":
        return H("t1", 0) + H("t1", 1)
    if k == "r1":
        return A("r1", 0) + A("r1", 1)
    if k in ("lg0", "lg1"):
        return A(k)
    if k == "cha":
        return ([("dl", ("sm",), 1), ("ed", ("sm",), 1)] if step[1] == 1 else []) + [("dl", step, 1), ("ed", step, 1)]
    if k == "chb":
        return [("wts", step, 1), ("A", ("wT", step[1]), 1)]
    if k == "chc":
        return [("A", ("b", step[1], hf), 1) for hf in range(2)]
    if k == "up0":
        return H(*step)
    if k == "down0":
        return Y("y0", step[1]) if step[2] == HTILES - 1 else []
    if k == "s":
        return [("A", step, 1)]
    if k == "mparts":
        return [("mp", step, 1)]
    if k == "mT":
        return Y("mT", 0) + Y("mT", 1) + [("ms", step, 16 * PARTS)]
    if k == "st":
        return [("A", (*step, pr), 1) for pr in range(2)]
    if k == "av":
        return Y("av", step[1], step[2]) if step[3] == TILES - 1 else []
    if k == "fin":
        return H("ctx", step[1], step[2])
    if k == "proj":
        return H("ctxT", step[1]) + H("proj", step[1])
    if k in ("u1", "u2"):
        return H(*step)
    if k == "y1":
        return Y(*step)
    if k == "store":
        return [("out", step, 16)]
    return []


BANKS = {"A": 2, "H": 2, "Y": 2}


class Pass:

    def __init__(self, before, att, unit, near, load):
        self.att, self.unit, self.near, self.load = att, unit, near, load
        self.steps = schedule(att, unit, near, load)
        self.start = dict(before)
        self.place, self.bank, ring = {}, {}, dict(before["ring"])
        count = {}
        for step in self.steps:
            for name, key, much in signals(step):
                if name in BANKS:
                    n = ring.get(name, 0)
                    ring[name] = n + 1
                    self.bank[key] = f"{name}{n % BANKS[name]}"
                    name = "bank"
                    count[self.bank[key]] = count.get(self.bank[key], 0) + 1
                    self.place[name, key] = count[self.bank[key]]
                else:
                    count[name] = count.get(name, 0) + much
                    self.place[name, key] = count[name]
        self.count = count
        self.ring = ring

    def after(self, times):
        if times > 1:
            assert all((self.ring[n] - self.start["ring"].get(n, 0)) % BANKS[n] == 0 for n in self.ring)
        end = {n: self.start.get(n, 0) + times * c for n, c in self.count.items()}
        return {**self.start, **end, "ring": self.ring}


def graph_kernel(nc, x, adj, gW, gb, Wg, bg, W1, b1, W2, b2, Wq, Wk, Wv, Wo, bo,
                 rw1, rb1, rw2, rb2, ew1, eb1, ew2, eb2, ew3, eb3, out):
    ctx = ExitStack()
    with ctx:
        def sb(name, shape, dt=F32):
            return ctx.enter_context(nc.sbuf_tensor(name, shape, dt))

        def sem(name):
            return ctx.enter_context(nc.semaphore(name))

        table = nc.dram_tensor("table", (ROWS, C), F32, kind="Internal").ap()
        parts_dram = nc.dram_tensor("parts_dram", (2, PARTS, P, NODES), BF16, kind="Internal").ap()

        gW_sb = sb("gW_sb", [P, 2, C])
        Wg_sb = sb("Wg_sb", [P, E0])
        W1_sb = sb("W1_sb", [P, E0, HID0])
        W2_sb = sb("W2_sb", [P, E0, HC, C])
        Wat_sb = sb("Wat_sb", [P, 4, C])
        rw1_sb = sb("rw1_sb", [P, RH])
        rw2_sb = sb("rw2_sb", [RH, E1])
        ew_sb = sb("ew_sb", [P, 3, E1, C])
        gb_b = sb("gb_b", [P, C])
        bo_b = sb("bo_b", [P, C])
        bg_b = sb("bg_b", [P, E0])
        rb2_b = sb("rb2_b", [P, E1])
        bias_T = sb("bias_T", [P, P])
        EB1, EB2, RB1 = E0 * HC, E0 * HC + E1, E0 * HC + 2 * E1
        bias_diag = sb("bias_diag", [2 * TILES * EP, HTILES, C])
        ident = sb("ident", [P, P])
        identb = sb("identb", [P, P], BF16)
        countdown = sb("countdown", [P, NODES], F16)
        eidx = sb("eidx", [P, TILES, EP])
        ones = sb("ones", [P, 1])
        less = sb("less", [P, 2])
        pool_pad = sb("pool_pad", [1, 4])
        dve_pad = sb("dve_pad", [1, 4])

        xn0 = sb("xn0", [P, TILES, C])
        adj_sb = sb("adj_sb", [P, 2, NODES], I32)
        score = sb("score", [P, NODES], F16)
        edges = sb("edges", [P, NODES], U8)
        degree = sb("degree", [P, 1])
        excess = sb("excess", [P, 2])
        above = sb("above", [1, 2])
        above_sum = sb("above_sum", [1, 1])
        degree_class = sb("degree_class", [1, TILES], I32)
        top = sb("top", [P, 2, TOP])
        slot_idx = sb("slot_idx", [P, TILES, SLOTS], U32)
        floor = sb("floor", [P, TILES])
        keeps = [sb(f"keep{i}", [P, TILES]) for i in range(3)]
        G = sb("G", [P, 2, SLOTS, C])
        agg = sb("agg", [P, TILES, C])
        res_b = sb("res_b", [P, TILES, C])
        res_n = sb("res_n", [P, TILES, C])
        xn = sb("xn", [P, TILES, C])
        XT = sb("XT", [P, NODES])
        XT2 = sb("XT2", [P, NODES])
        XB = sb("XB", [P, NODES])
        st = sb("st", [P, TILES, 6])
        mv = sb("mv", [P, TILES, 2])
        sd = sb("sd", [P, TILES])
        sq = sb("sq", [P, TILES])
        rstd = sb("rstd", [P, TILES])
        lg = sb("lg", [P, TILES, EP])
        ex = sb("ex", [P, TILES, EP])
        pr_sb = sb("pr_sb", [P, TILES, EP])
        best = sb("best", [P, TILES, EP])
        besti = sb("besti", [P, TILES, EP], U32)
        bestf = sb("bestf", [P, TILES, EP])
        dlt = sb("dlt", [P, TILES])
        ed = sb("ed", [P, TILES])
        w1st = sb("w1st", [P, TILES])
        w2nd = sb("w2nd", [P, TILES])
        pick = sb("pick", [P, 2, TILES, EP])
        wts = [sb(f"wts{i}", [P, P // EP, EP]) for i in range(2)]
        WT = sb("WT", [2 * TILES * EP, P])
        tmp = sb("tmp", [P, HALF])
        bias_rows = tmp[:, 0:P]
        zrows = tmp[0:1, P:2 * P]
        HB = sb("HB", [P, 2, HC, HALF])
        adjm = sb("adjm", [P, NODES], I32)
        drop = sb("drop", [P, TILES])
        mask = sb("mask", [P, TILES, NODES], BF16)
        QS = sb("QS", [P, HEADS, NODES], BF16)
        KS = sb("KS", [P, HEADS, NODES], BF16)
        VS = sb("VS", [P, TILES, HEADS * (D + 1) + 32 - (D + 1)])
        VH = VS[:, :, 0:HEADS * (D + 1)].rearrange("p t (h e) -> p t h e", e=D + 1)
        parts = sb("parts", [P, PARTS, NODES], BF16)
        junk = parts[:, 0, :]
        MX = sb("MX", [P, HEADS, TILES])
        mrest = sb("mrest", [P, HEADS * TILES])
        mparts = sb("mparts", [P, PARTS, P], BF16)
        mT = sb("mT", [P, PARTS, P], BF16)
        rden = sb("rden", [P, HTILES, GH])
        res_f = mask[:, TILES // 2:TILES // 2 + 2, :].rearrange("p a n -> p (a n)").bitcast(F32).rearrange(
            "p (t c) -> p t c", c=C)
        XF = mask[:, 0:2, :].rearrange("p a n -> p (a n)").bitcast(F32)
        XQ = HB[:, 1, 0:2, :].rearrange("p a (t c) -> p (a t) c", c=C)
        rest = tmp
        CT = tmp
        ctxn = xn[:, 0:HTILES, :]

        ring_banks = {
            "A": [ctx.enter_context(nc.psum_tensor(f"PA{i}", [P, NODES], F32)) for i in range(2)],
            "H": [ctx.enter_context(nc.psum_tensor(f"PH{i}", [P, HALF], F32)) for i in range(2)],
            "Y": [ctx.enter_context(nc.psum_tensor(f"PY{i}", [P, HALF], F32)) for i in range(2)],
        }
        full = {f"{n}{i}": sem(f"psum_{n}{i}_full") for n, r in ring_banks.items() for i in range(len(r))}
        free = {f"{n}{i}": sem(f"psum_{n}{i}_free") for n, r in ring_banks.items() for i in range(len(r))}

        s_w = sem("weights_loaded")
        s_const = sem("constants_made")
        s_ident = sem("identity_zeroed")
        s_made = sem("vector_constants_made")
        s_btp = sem("bias_transposed")
        s_bt = sem("bias_columns_copied")
        S = {name: sem(words) for name, words in {
            "var": "variance_ready", "sq": "deviation_ready", "xn0": "normed_input_ready",
            "xn": "normed_ready", "x1": "gnn_done", "xin": "x_loaded",
            "took": "residual_taken", "resx": "residual_loaded", "tab": "table_stored",
            "adj0": "adjacency_loaded0", "adj1": "adjacency_loaded1", "adjf": "adjacency_used",
            "adjm": "mask_adjacency_loaded", "adjmf": "mask_adjacency_used",
            "idx": "slot_indices_ready", "gat0": "neighbours_fetched0", "gat1": "neighbours_fetched1",
            "dg": "degree_excess_ready", "cat": "degree_class_ready", "aggr": "aggregate_ready", "q1": "first_part_ready",
            "parts": "parts_ready", "pd": "parts_stored", "stack": "stacks_loaded",
            "dl": "router_input_ready", "ed": "router_exp_ready", "wts": "expert_weights_ready",
            "mp": "max_parts_ready", "ms": "max_rows_stacked", "out": "stored"}.items()}

        state = {n: 1 for n in free} | {"out": 16, "ring": {}}
        passes = []
        for g in range(-3, GRAPHS):
            parts_of = (g >= 0, 0 <= g + 1 < GRAPHS, 0 <= g + 2 < GRAPHS, g + 3 < GRAPHS)
            if g > 0 and all(parts_of):
                continue
            passes.append((g, Pass(state, *parts_of)))
            loops = GRAPHS - 3 if all(parts_of) else 1
            state = passes[-1][1].after(loops)

        def over_passes(eng, body):
            for g, ps in passes:
                if g == 0:
                    with eng.Fori(0, GRAPHS - 3) as b:
                        body(ps, b, b)
                else:
                    body(ps, 0, g)

        def reached(ps, turn, name, key=None):
            here = ps.place[name, key] if key is not None else 0
            return turn * ps.count.get(name, 0) + (ps.start.get(name, 0) + here)

        def at(ps, turn, name, key=None):
            return S[name], reached(ps, turn, name, key)

        def psum(ps, key):
            return ring_banks[ps.bank[key][0]][int(ps.bank[key][1])]

        def ring_place(ps, turn, key):
            name = ps.bank[key]
            return name, turn * ps.count[name] + (ps.start[name] + ps.place["bank", key])

        def is_free(ps, turn, key):
            name, v = ring_place(ps, turn, key)
            return free[name], v - 1

        def is_taken(ps, turn, key):
            name, v = ring_place(ps, turn, key)
            return free[name], v

        def is_full(ps, turn, key):
            name, v = ring_place(ps, turn, key)
            return full[name], v - 1

        def filled(ps, key):
            return full[ps.bank[key]], 1

        def emptied(ps, key):
            return free[ps.bank[key]], 1

        x_v = x.rearrange("b (t p) c -> b p t c", p=P)
        adj_v = adj.rearrange("b (t p) m -> b t p m", p=P)
        out_v = out.rearrange("b (t p) c -> b p t c", p=P)
        parts_v = parts_dram.rearrange("s k (h d) n -> s k d h n", d=D)
        half = [slice(0, HALF), slice(HALF, NODES)]
        htiles = [slice(0, HTILES), slice(HTILES, TILES)]
        block = ctx.enter_context(nc.Block())

        def held_by(eng, pad, pool=False):
            if pool:
                eng.tensor_tensor(pad[0:1, 0:1], pad[0:1, 1:2], pad[0:1, 2:3], ALU.add)
                eng.drain()
            else:
                eng.memset(pad[0:1, 0:1], 0.0)

        loads = [
            (gW_sb[:, :, :], gW.rearrange("(k p) c -> p k c", p=P)), (Wg_sb[:, :], Wg),
            (W1_sb[:, :, :], W1.rearrange("e p h -> p e h")),
            (W2_sb[:, :, :, :], W2.rearrange("e (k p) c -> p e k c", p=P)),
            (Wat_sb[:, 0, :], Wq), (Wat_sb[:, 1, :], Wk), (Wat_sb[:, 2, :], Wv), (Wat_sb[:, 3, :], Wo),
            (rw1_sb[:, :], rw1), (rw2_sb[:, :], rw2),
            (ew_sb[:, 0, :, :], ew1.rearrange("e p h -> p e h")),
            (ew_sb[:, 1, :, :], ew2.rearrange("e p h -> p e h")),
            (ew_sb[:, 2, :, :], ew3.rearrange("e p h -> p e h")),
            (gb_b[:, :], gb.partition_broadcast(P)), (bo_b[:, :], bo.partition_broadcast(P)),
            (bg_b[:, :], bg.partition_broadcast(P)), (rb2_b[:, :], rb2.partition_broadcast(P)),
        ]
        late_loads = [
            (bias_rows[0:E0 * HC, :], b1.rearrange("e (k p) -> (e k) p", p=P)),
            (bias_rows[EB1:EB1 + E1, :], eb1), (bias_rows[EB2:EB2 + E1, :], eb2),
            (bias_rows[RB1:RB1 + 1, 0:RH], rb1.rearrange("(a n) -> a n", a=1)),
        ]
        for t in range(TILES):
            late_loads.append((bias_diag[t * EP:t * EP + E0, t % HTILES, :], b2))
            late_loads.append((bias_diag[(TILES + t) * EP:(TILES + t) * EP + E1, t % HTILES, :], eb3))
        N_LOADS = 16 * (len(loads) + len(late_loads))
        N_CONST = 6

        @block.sync
        def _(sp):
            sp.wait_ge(s_const, N_CONST)
            sp.dma_start(table[NODES:ROWS, :], zrows).then_inc(S["out"], 16)

            def body(ps, turn, b):
                for step in ps.steps:
                    kind = step[0]
                    if kind == "load_x":
                        if ps.near:
                            sp.wait_ge(*is_taken(ps, turn, ("xn", 1)))
                        sp.dma_start(xn0[:, :, :], x_v[b + 3, :, :, :]).then_inc(S["xin"], 16)
                    elif kind == "load_w":
                        for dst, src in loads + late_loads:
                            sp.dma_start(dst, src).then_inc(s_w, 16)
                    elif kind == "load_res":
                        if ps.unit:
                            sp.wait_ge(*at(ps, turn, "took", ("take",)))
                        sp.dma_start(res_n[:, :, :], x_v[b + 2, :, :, :]).then_inc(S["resx"], 16)
                    elif kind == "store_x":
                        sp.wait_ge(*at(ps, turn, "xn0", ("ln", 0)))
                        sp.dma_start(table[0:NODES, :].rearrange("(t p) c -> p t c", p=P),
                                     xn0[:, :, :]).then_inc(S["tab"], 16)
                    elif kind == "load_adj":
                        t = step[1]
                        sp.wait_ge(*at(ps, turn, "adjf", ("find", t - 2)))
                        sp.dma_start(adj_sb[:, t % 2, :], adj_v[b + 2, t, :, :]).then_inc(S[f"adj{t % 2}"], 16)
                    elif kind == "next_adj":
                        t = step[1]
                        if ps.near:
                            sp.wait_ge(*at(ps, turn, "adjf", ("find", TILES - 2 + t)))
                        sp.dma_start(adj_sb[:, t, :], adj_v[b + 3, t, :, :]).then_inc(S[f"adj{t}"], 16)
                    elif kind == "load_mask":
                        t = step[1]
                        sp.wait_ge(*at(ps, turn, "adjmf", ("mask", t - 1)))
                        sp.dma_start(adjm[:, :], adj_v[b, t, :, :]).then_inc(S["adjm"], 16)
                    elif kind == "next_mask":
                        if ps.att:
                            sp.wait_ge(*at(ps, turn, "adjmf", ("mask", TILES - 1)))
                        sp.dma_start(adjm[:, :], adj_v[b + 1, 0, :, :]).then_inc(S["adjm"], 16)
                    elif kind == "qk":
                        i = step[1]
                        sp.wait_ge(*at(ps, turn, "parts", step))
                        sp.dma_start(parts_dram[i, :, :, :].rearrange("k p n -> p k n"),
                                     parts[:, :, :]).then_inc(S["pd"], 16)
                        sp.wait_ge(*at(ps, turn, "pd", step))
                        stack, which = ((QS, QPART), (KS, KPART))[i]
                        for j, k in enumerate(which):
                            sp.dma_start(stack[D * j:D * j + D, :, :],
                                         parts_v[i, k, :, :, :]).then_inc(S["stack"], 16)
                    elif kind == "mT":
                        sp.wait_ge(*is_taken(ps, turn, ("mT", 1)))
                        for k in range(PARTS):
                            sp.dma_start(QS[SROWS + k:SROWS + k + 1, :, :].rearrange("o h n -> o (h n)"),
                                         mT[0:HEADS * TILES, k, :]).then_inc(S["ms"], 16)
                    elif kind == "store":
                        sp.wait_ge(*is_taken(ps, turn, ("y1", len(ORDER1) - 1)))
                        sp.dma_start(out_v[b, :, :, :], res_f).then_inc(S["out"], 16)

            over_passes(sp, body)
            sp.wait_ge(S["out"], 16 * GRAPHS + 16)

        @block.gpsimd
        def _(pool):
            pool.memset(ident[:, :], 0.0).then_inc(s_ident, 1)
            pool.memset(identb[:, :], 0.0).then_inc(s_ident, 1)
            pool.memset(pool_pad[:, :], 0.0).then_inc(s_ident, 1)
            pool.memset(tmp[:, 0:2 * P], 0.0).then_inc(s_const, 1)
            pool.memset(bias_diag[:, :, :], 0.0).then_inc(s_const, 1)
            pool.iota(countdown[:, :], pattern=[[-1, NODES]], base=NODES, channel_multiplier=0,
                      allow_small_or_imprecise_dtypes=True).then_inc(s_const, 1)
            pool.iota(eidx[:, :, :], pattern=[[0, TILES], [1, EP]], base=0, channel_multiplier=0,
                      allow_small_or_imprecise_dtypes=True).then_inc(s_const, 1)
            pool.wait_ge(s_ident, 3)
            for m in (ident, identb):
                pool.affine_select(out=m[:, :], in_=m[:, :], compare_op=ALU.not_equal, fill=1.0,
                                   base=0, pattern=[[-1, P]], channel_multiplier=1).then_inc(s_const, 1)
            pool.wait_ge(s_const, N_CONST)
            pool.wait_ge(S["out"], 16)

            def body(ps, turn, b):
                if ps.near:
                    pool.wait_ge(*at(ps, turn, "tab"))
                    for t in range(TILES):
                        pool.wait_ge(*at(ps, turn, "idx", ("find", t)))
                        held_by(pool, pool_pad, True)
                        if t >= 2:
                            pool.wait_ge(*at(ps, turn, "aggr", ("pmax", t - 2)))
                            held_by(pool, pool_pad, True)

                        def fetch(s, times=1):
                            pool.indirect_dma_start(
                                G[:, t % 2, s, :], None, table,
                                bass.IndirectOffsetOnAxis(slot_idx[:, t, s:s + 1], axis=0),
                                bounds_check=ROWS - 1, oob_is_err=False).then_inc(S[f"gat{t % 2}"], 16 * times)

                        few, some = CLASS_SLOTS
                        which = pool.value_load(degree_class[0:1, t:t + 1], min_val=0, max_val=2)
                        for s in range(few - 2):
                            fetch(s)
                        with pool.If(which < 1):
                            fetch(few - 2, (SLOTS - few + 2) // 2)
                            fetch(few - 1, (SLOTS - few + 3) // 2)
                        with pool.If(which > 0):
                            for s in range(few - 2, some - 1):
                                fetch(s)
                            with pool.If(which < 2):
                                fetch(some - 1, SLOTS - some + 1)
                            with pool.If(which > 1):
                                for s in range(some - 1, SLOTS):
                                    fetch(s)

            over_passes(pool, body)

        @block.vector
        def _(dve):
            def settle(ins):
                dve.drain()
                return ins

            def moments(ps, turn, i):
                if i == 0:
                    dve.wait_ge(*at(ps, turn, "xin", ("load_x",)))
                src = (xn0, res_n, res_b, res_b)[i]
                for t in range(TILES):
                    dve.bn_stats(st[:, t, :], src[:, t, :])
                dve.drain()
                for t in range(TILES):
                    dve.bn_aggr(mv[:, t, :], st[:, t, :])
                dve.drain()
                settle(dve.tensor_scalar(sd[:, :], mv[:, :, 1], EPS, None, ALU.add).then_inc(S["var"], 1))

            def norm(ps, turn, step):
                i = step[1]
                src, dst = ((xn0, xn0), (res_n, xn), (res_b, xn), (res_b, xn))[i]
                if i == 1 and ps.unit:
                    dve.wait_ge(*is_taken(ps, turn, ("tq", 1)))
                    held_by(dve, dve_pad)
                if i == 2 and ps.att:
                    dve.wait_ge(*is_taken(ps, turn, ("t1", 1)))
                    held_by(dve, dve_pad)
                dve.wait_ge(*at(ps, turn, "sq", step))
                settle(dve.reciprocal(rstd[:, :], sq[:, :]))
                for t in range(TILES):
                    ins = dve.tensor_scalar(dst[:, t, :], src[:, t, :], mv[:, t, 0:1], rstd[:, t:t + 1],
                                            ALU.subtract, ALU.mult)
                if i == 2:
                    dve.drain()
                    for t in range(TILES):
                        ins = dve.tensor_scalar(XQ[:, t, :], xn[:, t, :], keeps[1][:, t:t + 1], None, ALU.mult)
                ins.then_inc(S["xn0" if i == 0 else "xn"], 1)
                dve.drain()

            def find(ps, turn, t):
                tp = top[:, t % 2, :]
                few, some = CLASS_SLOTS
                dve.wait_ge(*at(ps, turn, "cat", ("class", t)))
                held_by(dve, dve_pad[:, 2:3])
                which = dve.value_load(degree_class[0:1, t:t + 1], min_val=0, max_val=2)
                dve.wait_ge(*at(ps, turn, f"adj{t % 2}", ("load_adj", t) if t >= 2 else None))
                dve.scalar_tensor_tensor(out=score[:, :], in0=adj_sb[:, t % 2, :], scalar=0,
                                         in1=countdown[:, :], op0=ALU.not_equal,
                                         op1=ALU.mult).then_inc(S["adjf"], 1)
                settle(dve.memset(tp[:, few:TOP], 0.0))
                settle(dve.max(tp[:, 0:few], score[:, :]))
                with dve.If(which > 0):
                    settle(dve.match_replace(score[:, :], tp[:, 0:few], score[:, :], 0.0))
                    settle(dve.max(tp[:, few:some], score[:, :]))
                    with dve.If(which > 1):
                        for r in range(some // 8, ROUNDS):
                            settle(dve.match_replace(score[:, :], tp[:, 8 * r - 8:8 * r], score[:, :], 0.0))
                            settle(dve.max(tp[:, 8 * r:8 * r + 8], score[:, :]))
                dve.tensor_scalar(slot_idx[:, t, :], tp[:, 0:SLOTS], -1.0, float(NODES),
                                  ALU.mult, ALU.add).then_inc(S["idx"], 1)
                dve.tensor_scalar(keeps[2][:, t:t + 1], tp[:, 0:1], 0.0, None, ALU.is_gt)
                settle(dve.tensor_scalar(floor[:, t:t + 1], tp[:, SLOTS:SLOTS + 1], 0.0, LOWEST,
                                         ALU.is_gt, ALU.mult))

            def pool_max(ps, turn, t):
                few, some = CLASS_SLOTS
                dve.wait_ge(*at(ps, turn, f"gat{t % 2}", ("pmax", t)))
                held_by(dve, dve_pad[:, 2:3])
                which = dve.value_load(degree_class[0:1, t:t + 1], min_val=0, max_val=2)

                def most(slots):
                    settle(dve.tensor_reduce(out=agg[:, t, :], in_=G[:, t % 2, 0:slots, :].rearrange("p s c -> p c s"),
                                             axis=AX.X, op=ALU.max))

                with dve.If(which < 1):
                    most(few)
                with dve.If(which > 0):
                    with dve.If(which < 2):
                        most(some)
                    with dve.If(which > 1):
                        most(SLOTS)
                settle(dve.tensor_scalar(agg[:, t, :], agg[:, t, :], floor[:, t:t + 1], None,
                                         ALU.max).then_inc(S["aggr"], 1))

            def gnn_add(ps, turn):
                dve.wait_ge(*at(ps, turn, "resx", ("load_res",)))
                held_by(dve, dve_pad)
                for hf in range(2):
                    key = ("gnn", hf)
                    dve.wait_ge(*is_full(ps, turn, key))
                    y = psum(ps, key)[:, :].rearrange("p (t c) -> p t c", c=C)
                    tm = tmp[:, :].rearrange("p (t c) -> p t c", c=C)
                    ins = dve.tensor_tensor(tm, y, gb_b[:, :].unsqueeze(1).to_broadcast([P, HTILES, C]), ALU.add)
                    ins.then_inc(*emptied(ps, key))
                    dve.drain()
                    ins = dve.scalar_tensor_tensor(out=res_n[:, htiles[hf], :], in0=tm, scalar=0.0,
                                                   in1=res_n[:, htiles[hf], :], op0=ALU.max, op1=ALU.add)
                    if hf == 1:
                        ins.then_inc(S["x1"], 1)
                    dve.drain()

            def two_best(ps, turn, step):
                layer = step[1]
                if layer == 0:
                    dve.wait_ge(*is_full(ps, turn, ("lg0",)))
                    ins = dve.tensor_tensor(lg[:, :, 0:E0],
                                            psum(ps, ("lg0",))[:, 0:TILES * E0].rearrange("p (t e) -> p t e", e=E0),
                                            bg_b[:, :].unsqueeze(1).to_broadcast([P, TILES, E0]), ALU.add)
                    ins.then_inc(*emptied(ps, ("lg0",)))
                    dve.drain()
                    values = lg
                else:
                    dve.wait_ge(*is_full(ps, turn, ("lg1",)))
                    ins = dve.tensor_tensor(lg[:, :, 0:E1],
                                            psum(ps, ("lg1",))[:, 0:TILES * E1].rearrange("p (t e) -> p t e", e=E1),
                                            rb2_b[:, :].unsqueeze(1).to_broadcast([P, TILES, E1]), ALU.add)
                    ins.then_inc(*emptied(ps, ("lg1",)))
                    dve.drain()
                    settle(dve.tensor_reduce(out=dlt[:, :], in_=lg[:, :, 0:E1], axis=AX.X, op=ALU.max))
                    settle(dve.tensor_tensor(lg[:, :, 0:E1], lg[:, :, 0:E1],
                                             dlt[:, :].unsqueeze(2).to_broadcast([P, TILES, E1]),
                                             ALU.subtract).then_inc(S["dl"], 1))
                    dve.wait_ge(*at(ps, turn, "ed", ("sm",)))
                    settle(dve.tensor_reduce(out=dlt[:, :], in_=ex[:, :, 0:E1], axis=AX.X, op=ALU.add))
                    settle(dve.reciprocal(dlt[:, :], dlt[:, :]))
                    settle(dve.tensor_tensor(pr_sb[:, :, 0:E1], ex[:, :, 0:E1],
                                             dlt[:, :].unsqueeze(2).to_broadcast([P, TILES, E1]), ALU.mult))
                    values = pr_sb
                for t in range(TILES):
                    dve.max(best[:, t, :], values[:, t, :])
                dve.drain()
                for t in range(TILES):
                    dve.max_index(besti[:, t, :], best[:, t, :], values[:, t, :])
                settle(dve.tensor_tensor(dlt[:, :], best[:, :, 1], best[:, :, 0],
                                         ALU.subtract).then_inc(S["dl"], 1))
                settle(dve.tensor_copy(bestf[:, :, 0:2], besti[:, :, 0:2]))
                for i in range(2):
                    dve.tensor_tensor(pick[:, i, :, :], eidx[:, :, :],
                                      bestf[:, :, i:i + 1].to_broadcast([P, TILES, EP]), ALU.is_equal)
                dve.drain()

            def weigh(ps, turn, step):
                layer = step[1]
                dve.wait_ge(*at(ps, turn, "ed", ("cha", layer)))
                settle(dve.tensor_scalar(w1st[:, :], ed[:, :], 1.0, None, ALU.add))
                settle(dve.reciprocal(w1st[:, :], w1st[:, :]))
                settle(dve.tensor_tensor(w2nd[:, :], ed[:, :], w1st[:, :], ALU.mult))
                for i, w in enumerate((w1st, w2nd)):
                    dve.tensor_tensor(pick[:, i, :, :], pick[:, i, :, :],
                                      w[:, :].unsqueeze(2).to_broadcast([P, TILES, EP]), ALU.mult)
                dve.drain()
                settle(dve.tensor_tensor(wts[layer][:, layer * TILES:(layer + 1) * TILES, :], pick[:, 0, :, :], pick[:, 1, :, :],
                                         ALU.add).then_inc(S["wts"], 1))

            def add_biases(ps, turn, step):
                layer = step[1]
                key = ("wT", layer)
                dve.wait_ge(*is_full(ps, turn, key))
                mine = slice(layer * TILES * EP, (layer + 1) * TILES * EP)
                dve.tensor_copy(WT[mine, :], psum(ps, key)[mine, 0:P]).then_inc(*emptied(ps, key))
                dve.drain()
                res = (res_n, res_f)[layer]
                for hf in range(2):
                    key = ("b", layer, hf)
                    dve.wait_ge(*is_full(ps, turn, key))
                    ins = dve.tensor_tensor(res[:, htiles[hf], :], res[:, htiles[hf], :],
                                            psum(ps, key)[:, 0:HALF].rearrange("p (t c) -> p t c", c=C), ALU.add)
                    ins.then_inc(*emptied(ps, key))
                dve.drain()

            def combine(ps, turn, layer, i):
                hf, e = (ORDER0, ORDER1)[layer][i]
                res = (res_n, res_f)[layer]
                key = (f"y{layer}", i)
                dve.wait_ge(*is_full(ps, turn, key))
                for tt in range(HTILES):
                    t = hf * HTILES + tt
                    ins = dve.scalar_tensor_tensor(out=res[:, t, :], in0=psum(ps, key)[:, tt * C:(tt + 1) * C],
                                                   scalar=wts[layer][:, layer * TILES + t, e:e + 1], in1=res[:, t, :],
                                                   op0=ALU.mult, op1=ALU.add)
                ins.then_inc(*emptied(ps, key))
                dve.drain()

            def split_parts(ps, turn, i):
                for hf in range(2):
                    cols = half[hf]
                    key = ("qk", i, hf)
                    dve.wait_ge(*at(ps, turn, "q1", ("q1", i, hf)))
                    ins = dve.tensor_tensor(rest[:, :], psum(ps, key)[:, :], parts[:, 0, cols], ALU.subtract)
                    ins.then_inc(*emptied(ps, key))
                    dve.drain()
                    settle(dve.tensor_copy(parts[:, 1, cols], rest[:, :]))
                    ins = dve.tensor_tensor(parts[:, 2, cols], rest[:, :], parts[:, 1, cols], ALU.subtract)
                    if hf == 1:
                        ins.then_inc(S["parts"], 1)
                    dve.drain()

            dve.wait_ge(s_const, N_CONST)
            for bank in free.values():
                dve.memset(dve_pad[:, 0:1], 0.0).then_inc(bank, 1)
                dve.drain()
            dve.memset(VS[:, :, :], 0.0)
            dve.memset(KS[SROWS:SROWS + PARTS, :, :], 1.0)
            dve.memset(mparts[:, :, :], 0.0)
            dve.memset(lg[:, :, :], -1.0)
            dve.memset(ones[:, :], 1.0)
            for i in range(2):
                dve.memset(less[:, i:i + 1], -float(CLASS_SLOTS[i]))
            dve.memset(pr_sb[:, :, :], -1.0)
            for w in wts:
                dve.memset(w[:, :, :], 0.0)
            for k in keeps:
                dve.memset(k[:, :], 0.0)
            dve.drain()
            dve.memset(VH[:, :, :, D:D + 1], 1.0).then_inc(s_made, 1)
            dve.drain()

            def body(ps, turn, b):
                for step in ps.steps:
                    kind = step[0]
                    if kind == "lnv":
                        moments(ps, turn, step[1])
                    elif kind == "ln":
                        norm(ps, turn, step)
                    elif kind == "bias":
                        dve.wait_ge(s_btp, 1)
                        settle(dve.tensor_copy(bias_T[:, :], ring_banks["Y"][0][:, 0:P]).then_inc(s_bt, 1))
                    elif kind == "find":
                        find(ps, turn, step[1])
                    elif kind == "pmax":
                        pool_max(ps, turn, step[1])
                    elif kind == "gnn_add":
                        gnn_add(ps, turn)
                    elif kind == "cha":
                        two_best(ps, turn, step)
                    elif kind == "chb":
                        weigh(ps, turn, step)
                    elif kind == "chc":
                        add_biases(ps, turn, step)
                    elif kind == "acc0":
                        combine(ps, turn, 0, step[1])
                    elif kind == "acc1":
                        combine(ps, turn, 1, step[1])
                    elif kind == "shift":
                        for i in range(2):
                            settle(dve.tensor_copy(keeps[i][:, :], keeps[i + 1][:, :]))
                        settle(dve.tensor_scalar(drop[:, :], keeps[0][:, :], -BIG, None, ALU.mult))
                    elif kind == "x2":
                        settle(dve.tensor_copy(res_f, res_b[:, :, :]))
                    elif kind == "take":
                        settle(dve.tensor_copy(res_b[:, :, :], res_n[:, :, :]).then_inc(S["took"], 1))
                    elif kind == "qk":
                        split_parts(ps, turn, step[1])
                    elif kind == "mask":
                        t = step[1]
                        if t == TILES // 2:
                            dve.wait_ge(*at(ps, turn, "out"))
                            held_by(dve, dve_pad)
                        dve.wait_ge(*at(ps, turn, "adjm", ("load_mask", t) if t >= 1 else None))
                        settle(dve.tensor_scalar(mask[:, t, :], adjm[:, :], 0, drop[:, t:t + 1],
                                                 ALU.is_le, ALU.mult).then_inc(S["adjmf"], 1))
                    elif kind == "s":
                        _, t, h = step
                        dve.wait_ge(*is_full(ps, turn, step))
                        if (t, h) == (0, 0):
                            held_by(dve, dve_pad[:, 1:2])
                            dve.wait_ge(*at(ps, turn, "stack"))
                        held_by(dve, dve_pad)
                        ins = dve.tensor_tensor_reduce(out=junk, in0=psum(ps, step)[:, :], in1=mask[:, t, :],
                                                       scale=1.0, scalar=LOWEST, op0=ALU.add, op1=ALU.max,
                                                       accum_out=MX[:, h, t:t + 1])
                        ins.then_inc(*emptied(ps, step))
                        dve.drain()
                    elif kind == "mparts":
                        mx = MX[:, :, :].rearrange("p h t -> p (h t)")
                        settle(dve.tensor_scalar(mrest[:, :], mx, -1.0, None, ALU.mult))
                        for k in range(PARTS):
                            ins = dve.tensor_copy(mparts[:, k, 0:HEADS * TILES], mrest[:, :])
                            if k == PARTS - 1:
                                ins.then_inc(S["mp"], 1)
                            dve.drain()
                            if k < PARTS - 1:
                                settle(dve.tensor_tensor(mrest[:, :], mrest[:, :],
                                                         mparts[:, k, 0:HEADS * TILES], ALU.subtract))
                    elif kind == "mT":
                        for part, (lo, hi) in enumerate(((0, 2), (2, PARTS))):
                            key = ("mT", part)
                            dve.wait_ge(*is_full(ps, turn, key))
                            ins = dve.tensor_copy(mT[:, lo:hi, :].rearrange("p k n -> p (k n)"),
                                                  psum(ps, key)[:, :].bitcast(BF16)[:, 0:(hi - lo) * P])
                            ins.then_inc(*emptied(ps, key))
                        dve.drain()
                    elif kind == "fin":
                        _, qh, g = step
                        key = ("av", qh, g)
                        dve.wait_ge(*is_full(ps, turn, key))
                        dve.tensor_copy(CT[:, :], psum(ps, key)[:, :]).then_inc(*emptied(ps, key))
                        dve.drain()
                        key = ("ctx", qh, g)
                        dve.wait_ge(*is_full(ps, turn, key))
                        c4 = psum(ps, key)[:, :].rearrange("p (q h d) -> p q h d", h=GH, d=32)
                        settle(dve.reciprocal(rden[:, :, :], c4[:, :, :, D]))
                        cn = ctxn[:, :, g * GH * D:(g + 1) * GH * D].rearrange("p q (h d) -> p q h d", d=D)
                        ins = dve.tensor_tensor(cn, c4[:, :, :, 0:D],
                                                rden[:, :, :].unsqueeze(3).to_broadcast([P, HTILES, GH, D]), ALU.mult)
                        ins.then_inc(*emptied(ps, key))
                        dve.drain()
                    elif kind == "proj":
                        qh = step[1]
                        key = ("proj", qh)
                        dve.wait_ge(*is_full(ps, turn, key))
                        y = psum(ps, key)[:, :].rearrange("p (t c) -> p t c", c=C)
                        ins = dve.tensor_tensor(res_b[:, htiles[qh], :], res_b[:, htiles[qh], :], y, ALU.add)
                        ins.then_inc(*emptied(ps, key))
                        dve.drain()
                        settle(dve.tensor_tensor(res_b[:, htiles[qh], :], res_b[:, htiles[qh], :],
                                                 bo_b[:, :].unsqueeze(1).to_broadcast([P, HTILES, C]), ALU.add))

            over_passes(dve, body)

        @block.scalar
        def _(act):
            def copy_out(dst, ps, turn, key):
                act.wait_ge(*is_full(ps, turn, key))
                act.activation(dst, psum(ps, key)[:, 0:HALF], ACT.Copy).then_inc(*emptied(ps, key))

            act.wait_ge(s_made, 1)

            def body(ps, turn, b):
                for step in ps.steps:
                    kind = step[0]
                    if kind == "deg":
                        t = step[1]
                        act.wait_ge(*at(ps, turn, f"adj{t % 2}", ("load_adj", t) if t >= 2 else None))
                        act.activation(edges[:, :], adj_sb[:, t % 2, :], ACT.Abs, accum_out=degree[:, :])
                        act.drain()
                        for i in range(2):
                            ins = act.activation(excess[:, i:i + 1], degree[:, :], ACT.Relu, bias=less[:, i:i + 1])
                        ins.then_inc(S["dg"], 1)
                    elif kind == "class":
                        t = step[1]
                        act.wait_ge(*is_full(ps, turn, step))
                        act.activation(above[:, :], psum(ps, step)[0:1, 0:2], ACT.Sign,
                                       accum_out=above_sum[:, :]).then_inc(*emptied(ps, step))
                        act.drain()
                        act.activation(degree_class[0:1, t:t + 1], above_sum[:, :], ACT.Copy).then_inc(S["cat"], 1)
                        act.drain()
                    elif kind == "lnv":
                        act.wait_ge(*at(ps, turn, "var", ("ln", step[1])))
                        act.activation(sq[:, :], sd[:, :], ACT.Sqrt).then_inc(S["sq"], 1)
                    elif kind == "gT":
                        for hf in range(2):
                            copy_out(XT[:, half[hf]], ps, turn, ("xn", hf))
                            copy_out(XT2[:, half[hf]], ps, turn, ("agg", hf))
                    elif kind == "qT":
                        for hf in range(2):
                            copy_out(XB[:, half[hf]], ps, turn, ("ta", hf))
                        for hf in range(2):
                            copy_out(XT2[:, half[hf]], ps, turn, ("tq", hf))
                    elif kind == "qk":
                        i = step[1]
                        for hf in range(2):
                            key = ("qk", i, hf)
                            act.wait_ge(*is_full(ps, turn, key))
                            if i == 1 and hf == 0:
                                act.wait_ge(*at(ps, turn, "pd", ("qk", 0)))
                            act.activation(parts[:, 0, half[hf]], psum(ps, key)[:, :],
                                           ACT.Copy).then_inc(S["q1"], 1)
                    elif kind == "v":
                        for hf in range(2):
                            key = ("v", hf)
                            act.wait_ge(*is_full(ps, turn, key))
                            act.activation(VH[:, htiles[hf], :, 0:D],
                                                   psum(ps, key)[:, 0:HALF].rearrange("p (t h d) -> p t h d", h=HEADS, d=D),
                                                   ACT.Copy).then_inc(*emptied(ps, key))
                    elif kind == "t0":
                        for hf in range(2):
                            copy_out(XT[:, half[hf]], ps, turn, ("t0", hf))
                    elif kind == "cha":
                        if step[1] == 1:
                            act.wait_ge(*at(ps, turn, "dl", ("sm",)))
                            act.activation(ex[:, :, 0:E1], lg[:, :, 0:E1], ACT.Exp).then_inc(S["ed"], 1)
                        act.wait_ge(*at(ps, turn, "dl", step))
                        act.activation(ed[:, :], dlt[:, :], ACT.Exp).then_inc(S["ed"], 1)
                    elif kind == "up0":
                        _, i, c = step
                        hf, e = ORDER0[i]
                        act.wait_ge(*is_full(ps, turn, step))
                        act.activation(HB[:, i % 2, c, :], psum(ps, step)[:, :], ACT.Gelu,
                                               bias=bias_T[:, e * HC + c:e * HC + c + 1]).then_inc(*emptied(ps, step))
                    elif kind == "st":
                        _, qh, g, kc = step
                        for pr in range(2):
                            key = (*step, pr)
                            act.wait_ge(*is_full(ps, turn, key))
                            act.activation(HB[:, kc % 2, 2 * pr:2 * pr + 2, :],
                                                   psum(ps, key)[:, :].rearrange("p (h q) -> p h q", h=2),
                                                   ACT.Exp, scale=float(D) ** -0.5).then_inc(*emptied(ps, key))
                    elif kind == "proj":
                        copy_out(XB[:, half[step[1]]], ps, turn, ("ctxT", step[1]))
                    elif kind == "t1":
                        for hf in range(2):
                            copy_out(XF[:, half[hf]], ps, turn, ("t1", hf))
                    elif kind == "r1":
                        for hf in range(2):
                            key = ("r1", hf)
                            act.wait_ge(*is_full(ps, turn, key))
                            act.activation(XB[0:RH, half[hf]], psum(ps, key)[0:RH, 0:HALF], ACT.Relu,
                                                   bias=bias_T[0:RH, RB1:RB1 + 1]).then_inc(*emptied(ps, key))
                    elif kind in ("u1", "u2"):
                        j = step[1]
                        hf, e = ORDER1[j]
                        act.wait_ge(*is_full(ps, turn, step))
                        k, col = (0, EB1) if kind == "u1" else (2, EB2)
                        act.activation(HB[:, 0, k + j % 2, :], psum(ps, step)[:, :], ACT.Relu,
                                               bias=bias_T[:, col + e:col + e + 1]).then_inc(*emptied(ps, step))

            over_passes(act, body)

        @block.tensor
        def _(pe):
            def transposes(ps, turn, key, src, hf):
                pe.wait_ge(*is_free(ps, turn, key))
                for tt in range(HTILES):
                    ins = pe.transpose(psum(ps, key)[:, tt * P:(tt + 1) * P], src[:, hf * HTILES + tt, :], ident[:, :])
                ins.then_inc(*filled(ps, key))

            def rows_times(ps, turn, key, srcT, hf, weight):
                pe.wait_ge(*is_free(ps, turn, key))
                for tt in range(HTILES):
                    t = hf * HTILES + tt
                    ins = pe.matmul(psum(ps, key)[:, tt * C:(tt + 1) * C], srcT[:, t * P:(t + 1) * P], weight,
                                    start=True, stop=True)
                ins.then_inc(*filled(ps, key))

            def body(ps, turn, b):
                for step in ps.steps:
                    kind = step[0]
                    if kind == "class":
                        pe.wait_ge(*at(ps, turn, "dg", ("deg", step[1])))
                        pe.wait_ge(*is_free(ps, turn, step))
                        pe.matmul(psum(ps, step)[0:1, 0:2], ones[:, :], excess[:, :],
                                  start=True, stop=True).then_inc(*filled(ps, step))
                    elif kind == "bias":
                        pe.wait_ge(s_w, N_LOADS)
                        pe.wait_ge(s_const, N_CONST)
                        pe.transpose(ring_banks["Y"][0][:, 0:P], bias_rows, ident[:, :]).then_inc(s_btp, 1)
                        pe.wait_ge(s_bt, 1)
                    elif kind == "gT":
                        pe.wait_ge(*at(ps, turn, "xn0"))
                        pe.wait_ge(*at(ps, turn, "aggr", ("pmax", TILES - 1)))
                        for hf in range(2):
                            transposes(ps, turn, ("xn", hf), xn0, hf)
                            transposes(ps, turn, ("agg", hf), agg, hf)
                    elif kind == "gnn":
                        for hf in range(2):
                            pe.wait_ge(*is_taken(ps, turn, ("xn", hf)))
                            pe.wait_ge(*is_taken(ps, turn, ("agg", hf)))
                            key = ("gnn", hf)
                            pe.wait_ge(*is_free(ps, turn, key))
                            for tt in range(HTILES):
                                t = hf * HTILES + tt
                                o = psum(ps, key)[:, tt * C:(tt + 1) * C]
                                pe.matmul(o, XT[:, t * P:(t + 1) * P], gW_sb[:, 0, :], start=True, stop=False)
                                ins = pe.matmul(o, XT2[:, t * P:(t + 1) * P], gW_sb[:, 1, :], start=False, stop=True)
                            ins.then_inc(*filled(ps, key))
                    elif kind == "qT":
                        pe.wait_ge(*at(ps, turn, "xn", ("ln", 2)))
                        for hf in range(2):
                            transposes(ps, turn, ("ta", hf), xn, hf)
                        for hf in range(2):
                            transposes(ps, turn, ("tq", hf), XQ, hf)
                    elif kind == "qk":
                        i = step[1]
                        src = (XT2, XB)[i]
                        for hf in range(2):
                            if i == 0:
                                pe.wait_ge(*is_taken(ps, turn, ("tq", hf)))
                            key = ("qk", i, hf)
                            pe.wait_ge(*is_free(ps, turn, key))
                            pe.matmul(psum(ps, key)[:, :], Wat_sb[:, i, :], src[:, half[hf]],
                                             start=True, stop=True).then_inc(*filled(ps, key))
                    elif kind == "v":
                        for hf in range(2):
                            rows_times(ps, turn, ("v", hf), XB, hf, Wat_sb[:, 2, :])
                    elif kind == "t0":
                        pe.wait_ge(*at(ps, turn, "xn", ("ln", 1)))
                        for hf in range(2):
                            transposes(ps, turn, ("t0", hf), xn, hf)
                    elif kind == "lg0":
                        pe.wait_ge(*is_taken(ps, turn, ("t0", 0)))
                        pe.wait_ge(*is_taken(ps, turn, ("t0", 1)))
                        pe.wait_ge(*is_free(ps, turn, ("lg0",)))
                        for t in range(TILES):
                            ins = pe.matmul(psum(ps, ("lg0",))[:, t * E0:(t + 1) * E0], XT[:, t * P:(t + 1) * P],
                                            Wg_sb[:, :], start=True, stop=True)
                        ins.then_inc(*filled(ps, ("lg0",)))
                    elif kind == "chb":
                        layer = step[1]
                        pe.wait_ge(*at(ps, turn, "wts", step))
                        key = ("wT", layer)
                        pe.wait_ge(*is_free(ps, turn, key))
                        pe.transpose(psum(ps, key)[:, 0:P], wts[layer][:, :, :].rearrange("p t e -> p (t e)"),
                                     ident[:, :]).then_inc(*filled(ps, key))
                    elif kind == "chc":
                        layer = step[1]
                        pe.wait_ge(*is_taken(ps, turn, ("wT", layer)))
                        for hf in range(2):
                            key = ("b", layer, hf)
                            pe.wait_ge(*is_free(ps, turn, key))
                            first_row = (2 * layer + hf) * HTILES * EP
                            rows = slice(first_row, first_row + HTILES * EP)
                            pe.matmul(psum(ps, key)[:, 0:HALF], WT[rows, :],
                                      bias_diag[rows, :, :].rearrange("k t c -> k (t c)"),
                                      start=True, stop=True).then_inc(*filled(ps, key))
                    elif kind == "up0":
                        _, i, c = step
                        hf, e = ORDER0[i]
                        pe.wait_ge(*is_free(ps, turn, step))
                        pe.matmul(psum(ps, step)[:, :], W1_sb[:, e, c * P:(c + 1) * P], XT[:, half[hf]],
                                         start=True, stop=True).then_inc(*filled(ps, step))
                    elif kind == "down0":
                        _, i, tt = step
                        hf, e = ORDER0[i]
                        key = ("y0", i)
                        if tt == 0:
                            for c in (HC - 2, HC - 1):
                                pe.wait_ge(*is_taken(ps, turn, ("up0", i, c)))
                            pe.wait_ge(*is_free(ps, turn, key))
                        for c in range(HC):
                            ins = pe.matmul(psum(ps, key)[:, tt * C:(tt + 1) * C],
                                            HB[:, i % 2, c, tt * P:(tt + 1) * P], W2_sb[:, e, c, :],
                                            start=(c == 0), stop=(c == HC - 1))
                        if tt == HTILES - 1:
                            ins.then_inc(*filled(ps, key))
                    elif kind == "s":
                        _, t, h = step
                        if (t, h) == (0, 0):
                            pe.wait_ge(*at(ps, turn, "stack"))
                        pe.wait_ge(*is_free(ps, turn, step))
                        for hf in range(2):
                            ins = pe.matmul(psum(ps, step)[:, half[hf]], QS[0:SROWS, h, t * P:(t + 1) * P],
                                            KS[0:SROWS, h, half[hf]], start=True, stop=True)
                        ins.then_inc(*filled(ps, step))
                    elif kind == "mT":
                        pe.wait_ge(*at(ps, turn, "mp", ("mparts",)))
                        for part, (lo, hi) in enumerate(((0, 2), (2, PARTS))):
                            key = ("mT", part)
                            pe.wait_ge(*is_free(ps, turn, key))
                            for k in range(lo, hi):
                                ins = pe.transpose(psum(ps, key)[:, :].bitcast(BF16)[:, (k - lo) * P:(k - lo + 1) * P],
                                                   mparts[:, k, :], identb[:, :])
                            ins.then_inc(*filled(ps, key))
                    elif kind == "st":
                        _, qh, g, kc = step
                        if (qh, g, kc) == (0, 0, 0):
                            pe.wait_ge(*at(ps, turn, "ms", ("mT",)))
                        for pr in range(2):
                            key = (*step, pr)
                            pe.wait_ge(*is_free(ps, turn, key))
                            for hh in range(2):
                                h = g * GH + 2 * pr + hh
                                o = psum(ps, key)[:, half[hh]]
                                pe.matmul(o, KS[0:SROWS + PARTS, h, kc * P:(kc + 1) * P],
                                          QS[0:SROWS + PARTS, h, half[qh]], start=True, stop=False)
                                for qt in range(HTILES):
                                    ins = pe.matmul(o[:, qt * P:(qt + 1) * P],
                                                    mask[:, qh * HTILES + qt, kc * P:(kc + 1) * P], identb[:, :],
                                                    start=False, stop=(qt == HTILES - 1))
                            ins.then_inc(*filled(ps, key))
                    elif kind == "av":
                        _, qh, g, kc = step
                        for pr in range(2):
                            pe.wait_ge(*is_taken(ps, turn, ("st", qh, g, kc, pr)))
                        key = ("av", qh, g)
                        if kc == 0:
                            pe.wait_ge(*is_free(ps, turn, key))
                        for hh in range(GH):
                            ins = pe.matmul(psum(ps, key)[32 * hh:32 * hh + 32, :], VS[:, kc, (D + 1) * (g * GH + hh):(D + 1) * (g * GH + hh) + 32],
                                            HB[:, kc % 2, hh, :], start=(kc == 0), stop=(kc == TILES - 1))
                        if kc == TILES - 1:
                            ins.then_inc(*filled(ps, key))
                    elif kind == "fin":
                        _, qh, g = step
                        pe.wait_ge(*is_taken(ps, turn, ("av", qh, g)))
                        key = ("ctx", qh, g)
                        pe.wait_ge(*is_free(ps, turn, key))
                        for tt in range(HTILES):
                            ins = pe.transpose(psum(ps, key)[:, tt * P:(tt + 1) * P], CT[:, tt * P:(tt + 1) * P],
                                               ident[:, :])
                        ins.then_inc(*filled(ps, key))
                    elif kind == "proj":
                        qh = step[1]
                        pe.wait_ge(*is_taken(ps, turn, ("ctx", qh, 0)))
                        pe.wait_ge(*is_taken(ps, turn, ("ctx", qh, 1)))
                        transposes(ps, turn, ("ctxT", qh), ctxn, 0)
                        pe.wait_ge(*is_taken(ps, turn, ("ctxT", qh)))
                        rows_times(ps, turn, ("proj", qh), XB, qh, Wat_sb[:, 3, :])
                    elif kind == "t1":
                        pe.wait_ge(*at(ps, turn, "xn", ("ln", 3)))
                        for hf in range(2):
                            transposes(ps, turn, ("t1", hf), xn, hf)
                    elif kind == "r1":
                        for hf in range(2):
                            pe.wait_ge(*is_taken(ps, turn, ("t1", hf)))
                            key = ("r1", hf)
                            pe.wait_ge(*is_free(ps, turn, key))
                            pe.matmul(psum(ps, key)[0:RH, 0:HALF], rw1_sb[:, :], XF[:, half[hf]],
                                             start=True, stop=True).then_inc(*filled(ps, key))
                    elif kind == "lg1":
                        pe.wait_ge(*is_taken(ps, turn, ("r1", 0)))
                        pe.wait_ge(*is_taken(ps, turn, ("r1", 1)))
                        pe.wait_ge(*is_free(ps, turn, ("lg1",)))
                        for t in range(TILES):
                            ins = pe.matmul(psum(ps, ("lg1",))[:, t * E1:(t + 1) * E1], XB[0:RH, t * P:(t + 1) * P],
                                            rw2_sb[:, :], start=True, stop=True)
                        ins.then_inc(*filled(ps, ("lg1",)))
                    elif kind == "u1":
                        hf, e = ORDER1[step[1]]
                        pe.wait_ge(*is_free(ps, turn, step))
                        pe.matmul(psum(ps, step)[:, :], ew_sb[:, 0, e, :], XF[:, half[hf]],
                                         start=True, stop=True).then_inc(*filled(ps, step))
                    elif kind == "u2":
                        j = step[1]
                        hf, e = ORDER1[j]
                        pe.wait_ge(*is_taken(ps, turn, ("u1", j)))
                        pe.wait_ge(*is_free(ps, turn, step))
                        pe.matmul(psum(ps, step)[:, :], ew_sb[:, 1, e, :], HB[:, 0, j % 2, :],
                                         start=True, stop=True).then_inc(*filled(ps, step))
                    elif kind == "y1":
                        j = step[1]
                        hf, e = ORDER1[j]
                        pe.wait_ge(*is_taken(ps, turn, ("u2", j)))
                        pe.wait_ge(*is_free(ps, turn, step))
                        for tt in range(HTILES):
                            ins = pe.matmul(psum(ps, step)[:, tt * C:(tt + 1) * C],
                                            HB[:, 0, 2 + j % 2, tt * P:(tt + 1) * P], ew_sb[:, 2, e, :],
                                            start=True, stop=True)
                        ins.then_inc(*filled(ps, step))

            over_passes(pe, body)


_INS = ['x', 'adj', 'L0_gnn_W', 'L0_gnn_b', 'L0_ffn_Wg', 'L0_ffn_bg', 'L0_ffn_W1', 'L0_ffn_b1', 'L0_ffn_W2',
        'L0_ffn_b2', 'L1_gnn_Wq', 'L1_gnn_Wk', 'L1_gnn_Wv', 'L1_gnn_Wo', 'L1_gnn_bo', 'L1_ffn_router_w1',
        'L1_ffn_router_b1', 'L1_ffn_router_w2', 'L1_ffn_router_b2', 'L1_ffn_expert_w1', 'L1_ffn_expert_b1',
        'L1_ffn_expert_w2', 'L1_ffn_expert_b2', 'L1_ffn_expert_w3', 'L1_ffn_expert_b3']


def kernel(**inputs):
    import numpy as np
    import concourse.bacc as bacc
    from concourse.bass_utils import run_bass_kernel_spmd

    nc = bacc.Bacc("TRN2", target_bir_lowering=False, num_devices=1)
    arrays, args = {}, []
    for name in _INS:
        a = np.ascontiguousarray(inputs[name])
        arrays[f"in_{name}"] = a
        args.append(nc.dram_tensor(f"in_{name}", a.shape, mybir.dt.from_np(a.dtype), kind="ExternalInput").ap())
    out = nc.dram_tensor("out_x", (GRAPHS, NODES, C), F32, kind="ExternalOutput").ap()
    graph_kernel(nc, *args, out)
    r = run_bass_kernel_spmd(nc, [arrays], core_ids=[0])
    return r.results[0]["out_x"]
```
